# Optimizing a Trainium2 kernel written in Bass

```python
import numpy as np
import jax
import jax.numpy as jnp

def _softmax(x, axis=-1):
    return jax.nn.softmax(x, axis=axis)

def _gelu(x):
    return jax.nn.gelu(x, approximate=True)

def _silu(x):
    return jax.nn.silu(x)

def _sigmoid(x):
    return jax.nn.sigmoid(x)

def _layernorm(x, axis=-1, eps=1e-05):
    m = jnp.mean(x, axis=axis, keepdims=True)
    v = jnp.var(x, axis=axis, keepdims=True)
    return (x - m) / jnp.sqrt(v + eps)

def _scatter_add(tgt, idx, src, axis=0):
    return tgt.at[idx].add(src)

def _segment_sum(src, seg, n):
    return jax.ops.segment_sum(src, seg, n)
kernel_name = 'mk_adj_ffn_d1_adj_r2_3fc292'

def setup_inputs(seed: int=0):
    np.random.seed(seed)
    _w = jnp.asarray

    def _rec_inputs():
        import jax
        import jax.numpy as jnp
        _gk = jax.random.key(seed)
        x = -0.0002928 + 1 * jax.random.normal(jax.random.fold_in(_gk, 1), (64, 128, 128), jnp.float32)
        _w = (1.0 + jnp.arange(128, dtype=jnp.float32)) ** (-0.5)
        _w = _w / _w.mean()
        _pij = jnp.clip(0.03125 * _w[:, None] * _w[None, :], 0.0, 1.0)
        _a = jax.random.uniform(jax.random.fold_in(_gk, 2), (64, 128, 128)) < _pij
        adj = _a.astype(jnp.int32)
        return (x, adj)
    x, adj = _rec_inputs()

    def _L0_gnn_setup():
        import jax, jax.numpy as jnp
        import numpy as np
        NEG_INF = -1000000000.0
        N_HEADS = 4

        def _graph_mha(x, adj_mask, Wq, bq, Wk, bk, Wv, bv):
            B, N, _ = x.shape
            Hd = Wq.shape[1]
            d = Hd // N_HEADS
            q = (x @ Wq + bq).reshape(B, N, N_HEADS, d)
            k = (x @ Wk + bk).reshape(B, N, N_HEADS, d)
            v = (x @ Wv + bv).reshape(B, N, N_HEADS, d)
            scale = 1.0 / d ** 0.5
            scores = jnp.einsum('bqhd,bkhd->bhqk', q, k) * scale
            scores = jnp.where(adj_mask[:, None, :, :], scores, NEG_INF)
            attn = jax.nn.softmax(scores, axis=-1)
            out = jnp.einsum('bhqk,bkhd->bqhd', attn, v).reshape(B, N, Hd)
            return out
        key = jax.random.key(seed)
        ks = jax.random.split(key, 16)
        B, N, D = (16, 512, 128)
        s = 0.05
        inp = {'nodes_embed': jax.random.normal(ks[0], (B, N, D), jnp.float32), 'node_adj': jax.random.randint(ks[1], (B, N, N), 0, 2, jnp.int32), 'Wq0': jax.random.normal(ks[2], (D, D), jnp.float32) * s, 'bq0': jnp.zeros((D,), jnp.float32), 'Wk0': jax.random.normal(ks[3], (D, D), jnp.float32) * s, 'bk0': jnp.zeros((D,), jnp.float32), 'Wv0': jax.random.normal(ks[4], (D, D), jnp.float32) * s, 'bv0': jnp.zeros((D,), jnp.float32), 'Wq1': jax.random.normal(ks[5], (2 * D, D), jnp.float32) * s, 'bq1': jnp.zeros((D,), jnp.float32), 'Wk1': jax.random.normal(ks[6], (2 * D, D), jnp.float32) * s, 'bk1': jnp.zeros((D,), jnp.float32), 'Wv1': jax.random.normal(ks[7], (2 * D, D), jnp.float32) * s, 'bv1': jnp.zeros((D,), jnp.float32), 'Wout': jax.random.normal(ks[8], (3 * D, D), jnp.float32) * s, 'bout': jnp.zeros((D,), jnp.float32)}
        return inp
    _L0_gnn_all = _L0_gnn_setup()
    _L0_gnn_in = {k: v for k, v in _L0_gnn_all.items() if k in ('Wq0', 'bq0', 'Wk0', 'bk0', 'Wv0', 'bv0', 'Wq1', 'bq1', 'Wk1', 'bk1', 'Wv1', 'bv1', 'Wout', 'bout')}
    del _L0_gnn_all

    def _L0_ffn_setup():
        import jax, jax.numpy as jnp
        import numpy as np
        B, S, D, E, H, K = (4, 2048, 128, 8, 256, 2)
        key = jax.random.key(seed)
        ks = jax.random.split(key, 6)
        x = jax.random.normal(ks[0], (B, S, D), jnp.float32)
        Wg = jax.random.normal(ks[1], (D, E), jnp.float32) * 0.02
        bg = jnp.zeros((E,), jnp.float32)
        W1 = jax.random.normal(ks[2], (E, D, H), jnp.float32) * 0.02
        b1 = jnp.zeros((E, H), jnp.float32)
        W2 = jax.random.normal(ks[3], (E, H, D), jnp.float32) * 0.02
        b2 = jnp.zeros((E, D), jnp.float32)
        return {'x': x, 'Wg': Wg, 'bg': bg, 'W1': W1, 'b1': b1, 'W2': W2, 'b2': b2}
    _L0_ffn_all = _L0_ffn_setup()
    _L0_ffn_in = {k: v for k, v in _L0_ffn_all.items() if k in ('Wg', 'bg', 'W1', 'b1', 'W2', 'b2')}
    del _L0_ffn_all
    return {'x': x, 'adj': adj, 'L0_gnn_Wq0': _L0_gnn_in['Wq0'], 'L0_gnn_bq0': _L0_gnn_in['bq0'], 'L0_gnn_Wk0': _L0_gnn_in['Wk0'], 'L0_gnn_bk0': _L0_gnn_in['bk0'], 'L0_gnn_Wv0': _L0_gnn_in['Wv0'], 'L0_gnn_bv0': _L0_gnn_in['bv0'], 'L0_gnn_Wq1': _L0_gnn_in['Wq1'], 'L0_gnn_bq1': _L0_gnn_in['bq1'], 'L0_gnn_Wk1': _L0_gnn_in['Wk1'], 'L0_gnn_bk1': _L0_gnn_in['bk1'], 'L0_gnn_Wv1': _L0_gnn_in['Wv1'], 'L0_gnn_bv1': _L0_gnn_in['bv1'], 'L0_gnn_Wout': _L0_gnn_in['Wout'], 'L0_gnn_bout': _L0_gnn_in['bout'], 'L0_ffn_Wg': _L0_ffn_in['Wg'], 'L0_ffn_bg': _L0_ffn_in['bg'], 'L0_ffn_W1': _L0_ffn_in['W1'], 'L0_ffn_b1': _L0_ffn_in['b1'], 'L0_ffn_W2': _L0_ffn_in['W2'], 'L0_ffn_b2': _L0_ffn_in['b2']}

def reference(x, adj, L0_gnn_Wq0, L0_gnn_bq0, L0_gnn_Wk0, L0_gnn_bk0, L0_gnn_Wv0, L0_gnn_bv0, L0_gnn_Wq1, L0_gnn_bq1, L0_gnn_Wk1, L0_gnn_bk1, L0_gnn_Wv1, L0_gnn_bv1, L0_gnn_Wout, L0_gnn_bout, L0_ffn_Wg, L0_ffn_bg, L0_ffn_W1, L0_ffn_b1, L0_ffn_W2, L0_ffn_b2):
    import jax
    import jax.numpy as jnp

    def _L0_gnn_ref(nodes_embed, node_adj, Wq0, bq0, Wk0, bk0, Wv0, bv0, Wq1, bq1, Wk1, bk1, Wv1, bv1, Wout, bout):
        import jax, jax.numpy as jnp
        import numpy as np
        NEG_INF = -1000000000.0
        N_HEADS = 4

        def _graph_mha(x, adj_mask, Wq, bq, Wk, bk, Wv, bv):
            B, N, _ = x.shape
            Hd = Wq.shape[1]
            d = Hd // N_HEADS
            q = (x @ Wq + bq).reshape(B, N, N_HEADS, d)
            k = (x @ Wk + bk).reshape(B, N, N_HEADS, d)
            v = (x @ Wv + bv).reshape(B, N, N_HEADS, d)
            scale = 1.0 / d ** 0.5
            scores = jnp.einsum('bqhd,bkhd->bhqk', q, k) * scale
            scores = jnp.where(adj_mask[:, None, :, :], scores, NEG_INF)
            attn = jax.nn.softmax(scores, axis=-1)
            out = jnp.einsum('bhqk,bkhd->bqhd', attn, v).reshape(B, N, Hd)
            return out
        adj_mask = node_adj > 0
        h0 = _graph_mha(nodes_embed, adj_mask, Wq0, bq0, Wk0, bk0, Wv0, bv0)
        x1 = jnp.concatenate((nodes_embed, h0), axis=-1)
        h1 = _graph_mha(x1, adj_mask, Wq1, bq1, Wk1, bk1, Wv1, bv1)
        x2 = jnp.concatenate((x1, h1), axis=-1)
        out = jax.nn.relu(x2 @ Wout + bout)
        return out

    def _L0_ffn_ref(x, Wg, bg, W1, b1, W2, b2):
        import jax, jax.numpy as jnp
        import numpy as np
        B, S, D, E, H, K = (4, 2048, 128, 8, 256, 2)
        Bv, Sv, Dv = x.shape
        gate_scores = x @ Wg + bg
        _, idx = jax.lax.top_k(gate_scores, K)
        mask = jax.nn.one_hot(idx, E, dtype=x.dtype).sum(axis=-2)
        xf = x.reshape(-1, Dv)
        mf = mask.reshape(-1, E)
        h = jax.nn.gelu(jnp.einsum('td,edh->teh', xf, W1) + b1[None], approximate=False)
        y = jnp.einsum('teh,ehd->ted', h, W2) + b2[None]
        out = jnp.einsum('ted,te->td', y, mf)
        return out.reshape(Bv, Sv, Dv)
    x = x + _L0_gnn_ref(_layernorm(x, axis=-1), adj, L0_gnn_Wq0, L0_gnn_bq0, L0_gnn_Wk0, L0_gnn_bk0, L0_gnn_Wv0, L0_gnn_bv0, L0_gnn_Wq1, L0_gnn_bq1, L0_gnn_Wk1, L0_gnn_bk1, L0_gnn_Wv1, L0_gnn_bv1, L0_gnn_Wout, L0_gnn_bout)
    x = x + _L0_ffn_ref(_layernorm(x, axis=-1), L0_ffn_Wg, L0_ffn_bg, L0_ffn_W1, L0_ffn_b1, L0_ffn_W2, L0_ffn_b2)
    return x

_drawn_inputs = setup_inputs


def setup_inputs(seed=0):
    import zlib

    import numpy as np

    out = dict(_drawn_inputs(seed))
    spreads = {'L0_gnn_bq0': (0.0, 0.738),
     'L0_gnn_bk0': (0.0, 0.8),
     'L0_gnn_bv0': (0.0, 0.1),
     'L0_gnn_bq1': (0.0, 0.756),
     'L0_gnn_bk1': (0.0, 0.8),
     'L0_gnn_bv1': (0.0, 0.1),
     'L0_gnn_bout': (0.0, 0.1),
     'L0_ffn_bg': (0.0, 0.1),
     'L0_ffn_b1': (0.0, 0.374),
     'L0_ffn_b2': (0.0, 0.1)}
    factors = {}
    for name, (base, spread) in spreads.items():
        noise = np.random.default_rng([zlib.crc32(name.encode()), seed]).standard_normal(out[name].shape)
        drawn = base * np.exp(spread * noise) if base else spread * noise
        out[name] = jnp.asarray(drawn.astype(out[name].dtype))
    for name, factor in factors.items():
        out[name] = (out[name] * factor).astype(out[name].dtype)
    return out
```

```python
from contextlib import ExitStack

import concourse.bass as bass
from concourse import mybir

F32 = mybir.dt.float32
F16 = mybir.dt.float16
BF16 = mybir.dt.bfloat16
I32 = mybir.dt.int32
U32 = mybir.dt.uint32
ALU = mybir.AluOpType
ACT = mybir.ActivationFunctionType
AX = mybir.AxisListType

P = 128
HEADS = 4
EPS = 1e-5
MASKED = -(2.0 ** 100)

LAG = {"A": 0, "B": 1, "C": 2}


def uses(order, stage, i, units):
    before = order.index(stage)
    if not isinstance(i, int):
        return len(order) * i - sum(LAG[s] for s in order) + before
    done = sum(min(max(i - LAG[s], 0), units) for s in order)
    return done + sum(0 <= i - LAG[s] < units for s in order[:before])


def gnn_moe_kernel(nc, x, adj, Wq0, bq0, Wk0, bk0, Wv0, bv0, Wq1, bq1, Wk1, bk1, Wv1, bv1,
                   Wout, bout, Wg, bg, W1, b1, W2, b2, out):
    B, T, D = x.shape
    E, _, HID = W1.shape
    assert T == P and D == P and HID == 2 * P and B % 8 == 0
    HD = D // HEADS
    U = 2
    UNITS = B // U
    TOK = U * T
    NC = HID // P
    NB1 = E * NC
    G = 4
    GROUPS = B // G
    GT = G * T
    XCH = 8

    with ExitStack() as ctx:
        def sb(name, shape, dt=F32):
            return ctx.enter_context(nc.sbuf_tensor(name, shape, dt))

        def pb(name, shape=(P, 512), dt=F32):
            return ctx.enter_context(nc.psum_tensor(name, list(shape), dt))

        def sem(name):
            return ctx.enter_context(nc.semaphore(name))

        ident = sb("ident", [P, P])
        ident_b = sb("ident_b", [P, P], BF16)
        iota8 = sb("iota8", [P, E])
        brows = sb("brows", [6 + NB1, P])
        bcols = sb("bcols", [P, 6 + NB1])
        bq = [bcols[:, 0:1], bcols[:, 1:2]]
        bk = [bcols[:, 2:3], bcols[:, 3:4]]
        bv = [bcols[:, 4:5], bcols[:, 5:6]]
        bout_bc = sb("bout_bc", [P, D])
        bg_bc = sb("bg_bc", [P, E])
        b2_f = sb("b2_f", [E, D])
        b2_hi = sb("b2_hi", [E, D], F16)
        b2_lo = sb("b2_lo", [E, D], BF16)
        wa_f = sb("wa_f", [P, 3, 3, D])
        wa_hi = sb("wa_hi", [P, 3, 3, D], F16)
        wa_lo = sb("wa_lo", [P, 3, 3, D], BF16)
        wo_f = sb("wo_f", [P, 3, D])
        wo_hi = sb("wo_hi", [P, 3, D], F16)
        wo_lo = sb("wo_lo", [P, 3, D], BF16)
        wg_f = sb("wg_f", [P, E])
        wg_hi = sb("wg_hi", [P, E], F16)
        wg_lo = sb("wg_lo", [P, E], BF16)
        w1_f = sb("w1_f", [P, E, HID])
        w1_hi = sb("w1_hi", [P, E, HID], F16)
        w1_lo = sb("w1_lo", [P, E, HID], BF16)
        w2_f = sb("w2_f", [P, E, NC, D])
        w2_hi = sb("w2_hi", [P, E, NC, D], F16)
        w2_lo = sb("w2_lo", [P, E, NC, D], BF16)

        held_p = sb("held_p", [P, 2])
        held_v = sb("held_v", [P, 2])

        xs = sb("xs", [P, B, D])
        st = [sb("st0", [P, B, 6]), sb("st1", [P, B, 6])]
        rstd = [sb("rstd0", [P, B]), sb("rstd1", [P, B])]
        nmr = [sb("nmr0", [P, B]), sb("nmr1", [P, B])]
        sa = sb("sa", [P, B])
        sbb = sb("sbb", [P, B])
        eps_c = sb("eps_c", [P, 1])

        adj_t = [sb(f"adj{p}", [P, U, T], I32) for p in range(2)]
        mask_b = [sb(f"mask{p}", [P, U, T], BF16) for p in range(2)]
        xn = [sb(f"xn{p}", [P, U, D]) for p in range(2)]
        xT = [sb(f"xT{p}", [P, 2, TOK], F16) for p in range(2)]
        xTk = [sb(f"xTk{p}", [P, 2, TOK], F16) for p in range(2)]
        h0T = [sb(f"h0T{p}", [P, 2, TOK], F16) for p in range(2)]
        h1T = sb("h1T", [P, 2, TOK], F16)
        qT = [sb(f"qT{l}", [P, 2, TOK], F16) for l in range(2)]
        kT = [sb(f"kT{l}", [P, 2, TOK], F16) for l in range(2)]
        v_hi = [sb(f"v_hi{l}", [P, U, HEADS, HD + 1], F16) for l in range(2)]
        v_lo = [sb(f"v_lo{l}", [P, U, HEADS, HD], F16) for l in range(2)]
        pr = [sb(f"pr{l}", [P, 2, 2 * U, T]) for l in range(2)]
        prT_hi = [sb(f"prT_hi{l}", [P, 2, 2 * U, T], F16) for l in range(2)]
        prT_lo = [sb(f"prT_lo{l}", [P, 2, 2 * U, T], F16) for l in range(2)]
        nmax = sb("nmax", [P, 2, 2, 2 * U])
        rden = sb("rden", [P, 2, U * HEADS])
        hn = [sb(f"hn{l}", [P, U, D]) for l in range(2)]
        og = sb("og", [P, U, D])

        xn2 = sb("xn2", [P, G, D])
        x2T = [sb(f"x2T{p}", [P, 2, GT], F16) for p in range(2)]
        gs = sb("gs", [P, G, E])
        top = sb("top", [P, G, 8])
        topi = sb("topi", [P, G, 8], U32)
        topf = sb("topf", [P, G, 2])
        eq = sb("eq", [P, 2, G, E])
        mk = [sb(f"mk{p}", [P, G, E]) for p in range(2)]
        mkT = sb("mkT", [E, GT], F16)
        hg = [sb(f"hg{p}", [P, NC, GT]) for p in range(2)]
        hg_hi = [sb(f"hg_hi{p}", [P, NC, GT], F16) for p in range(2)]
        hg_lo = [sb(f"hg_lo{p}", [P, NC, GT], F16) for p in range(2)]
        ym = [sb(f"ym{p}", [P, G, D]) for p in range(2)]
        acc = [sb(f"acc{p}", [P, G, D]) for p in range(2)]

        bX, bQ, bV, bO = pb("bX"), pb("bQ"), pb("bV"), pb("bO")
        bS = [pb(f"bS{j}") for j in range(2)]
        bT = [pb(f"bT{j}") for j in range(2)]

        x_in = [sem(f"x_in{k}") for k in range(XCH)]
        wa_in, wf_in, row_in, ffn_in = sem("wa_in"), sem("wf_in"), sem("row_in"), sem("ffn_in")
        adj_in = [sem(f"adj_in{p}") for p in range(2)]
        out_done = [sem("out_done0"), sem("out_done1")]
        iota_set, ident_set = sem("iota_set"), sem("ident_set")
        b_turned, b_ready = sem("b_turned"), sem("b_ready")
        prep = sem("prep")
        var_set, std_set = [sem("var0"), sem("var1")], [sem("std0"), sem("std1")]
        ln_ready = [sem("ln_ready0"), sem("ln_ready1")]
        ffn_hi_set = sem("ffn_hi_set")
        mask_set, xn_mul, xn_set, xT_kept = sem("mask_set"), sem("xn_mul"), sem("xn_set"), sem("xT_kept")
        X_fill, X_hi, X_empty = sem("X_fill"), sem("X_hi"), sem("X_empty")
        Q_fill, Q_hi, Q_empty = sem("Q_fill"), sem("Q_hi"), sem("Q_empty")
        V_fill, V_hi, V_empty = sem("V_fill"), sem("V_hi"), sem("V_empty")
        O_fill, O_rden, O_empty = sem("O_fill"), sem("O_rden"), sem("O_empty")
        S_fill = [sem(f"S_fill{j}") for j in range(2)]
        half_done = [sem(f"half_done{j}") for j in range(2)]
        S_max = [sem(f"S_max{j}") for j in range(2)]
        S_empty = [sem(f"S_empty{j}") for j in range(2)]
        T_fill = [sem(f"T_fill{j}") for j in range(2)]
        T_hi = [sem(f"T_hi{j}") for j in range(2)]
        T_empty = [sem(f"T_empty{j}") for j in range(2)]
        x2_set, st_set = sem("x2_set"), sem("st_set")

        OX, OQ, OV, OO, OS, OT = "ABC", "AB", "ABC", "BC", "AB", "BC"

        def n(order, stage, i):
            return uses(order, stage, i, UNITS)

        def steps(eng, body):
            for i in range(4):
                body(i, i % 2)
            with eng.Fori(4, UNITS - 1, 2) as i:
                body(i, 0)
                body(i + 1, 1)
            body(UNITS, UNITS % 2)
            body(UNITS + 1, (UNITS + 1) % 2)

        def active(stage, i):
            return not isinstance(i, int) or 0 <= i - LAG[stage] < UNITS

        def hold(eng, tile):
            eng.tensor_tensor(tile[:, 1:2], tile[:, 0:1], tile[:, 0:1], ALU.add)

        def split3(pairs):
            for (a_hi, a_lo), (b_hi, b_lo) in pairs:
                yield a_hi, b_hi
                yield a_hi, b_lo
                yield a_lo, b_hi

        def summed(dst, pairs):
            terms = list(split3(pairs))
            for m, (a, b) in enumerate(terms):
                last = nc.tensor.matmul(dst, a, b, start=(m == 0), stop=(m == len(terms) - 1))
            return last

        with nc.Block() as block:

            @block.sync
            def _(sp):
                per = B // XCH
                for k in range(XCH):
                    sp.dma_start(xs[:, k * per:(k + 1) * per, :],
                                 x[k * per:(k + 1) * per].rearrange("b t d -> t b d")).then_inc(x_in[k], 16)
                    if k == 0:
                        for u in range(2):
                            sp.dma_start(adj_t[u][:, :, :],
                                         adj[u * U:(u + 1) * U].rearrange("b t k -> t b k")).then_inc(adj_in[u], 16)
                with sp.Fori(2, UNITS - 1, 2) as i:
                    for p in range(2):
                        sp.wait_ge(mask_set, i + p - 1)
                        sp.dma_start(adj_t[p][:, :, :],
                                     adj[bass.ds((i + p) * U, U)].rearrange("b t k -> t b k")).then_inc(adj_in[p], 16)

            @block.gpsimd
            def _(pool):
                nc.gpsimd.memset(ident[:, :], 0.0).then_inc(ident_set, 1)
                nc.gpsimd.memset(held_p[:, :], 0.0).then_inc(ident_set, 1)
                pool.wait_ge(ident_set, 2)
                nc.gpsimd.affine_select(out=ident[:, :], in_=ident[:, :], compare_op=ALU.not_equal, fill=1.0,
                                        base=0, pattern=[[-1, P]], channel_multiplier=1).then_inc(ident_set, 1)
                pool.wait_ge(ident_set, 3)
                nc.gpsimd.tensor_copy(ident_b[:, :], ident[:, :]).then_inc(ident_set, 1)
                nc.gpsimd.iota(iota8[:, :], pattern=[[1, E]], base=0, channel_multiplier=0,
                               allow_small_or_imprecise_dtypes=True).then_inc(iota_set, 1)

                def pool_step(i, p):
                    if active("A", i):
                        if not isinstance(i, int) or i >= 2:
                            pool.wait_ge(S_fill[1], n(OS, "B", i - 1) + 1)
                            pool.wait_ge(X_fill, n(OX, "A", i - 2) + 1)
                        pool.wait_ge(adj_in[p], 16 * (i // 2 + 1) if isinstance(i, int) else 8 * (i - p) + 16)
                        pool.wait_ge(ln_ready[0], 1)
                        sl = bass.ds(i * U, U)
                        nc.gpsimd.tensor_tensor(xn[p][:, :, :], xs[:, sl, :],
                                                rstd[0][:, sl].unsqueeze(2).broadcast_to([P, U, D]),
                                                ALU.mult).then_inc(xn_mul, 1)
                        nc.gpsimd.tensor_scalar(mask_b[p][:, :, :], adj_t[p][:, :, :], 0.0, MASKED,
                                                ALU.is_le, ALU.mult).then_inc(mask_set, 1)
                        pool.wait_ge(xn_mul, i + 1)
                        nc.gpsimd.tensor_tensor(xn[p][:, :, :], xn[p][:, :, :],
                                                nmr[0][:, sl].unsqueeze(2).broadcast_to([P, U, D]),
                                                ALU.add).then_inc(xn_set, 1)
                        if not isinstance(i, int) or i >= 2:
                            pool.wait_ge(V_fill, n(OV, "C", i) + 1)
                        pool.wait_ge(X_empty, n(OX, "A", i) + 1)
                        hold(nc.gpsimd, held_p)
                        nc.gpsimd.tensor_copy(xTk[p][:, :, :].bitcast(F32),
                                              xT[p][:, :, :].bitcast(F32)).then_inc(xT_kept, 1)

                steps(pool, pool_step)
                pool.wait_ge(ffn_hi_set, 4)
                nc.gpsimd.tensor_tensor(w1_lo[:, :, :], w1_f[:, :, :], w1_hi[:, :, :], ALU.subtract)
                nc.gpsimd.tensor_tensor(w2_lo[:, :, :, :].rearrange("p e c d -> p (e c) d"),
                                        w2_f[:, :, :, :].rearrange("p e c d -> p (e c) d"),
                                        w2_hi[:, :, :, :].rearrange("p e c d -> p (e c) d"), ALU.subtract)
                nc.gpsimd.tensor_tensor(wg_lo[:, :], wg_f[:, :], wg_hi[:, :], ALU.subtract)
                nc.gpsimd.tensor_tensor(b2_lo[:, :], b2_f[:, :], b2_hi[:, :], ALU.subtract)

            @block.scalar
            def _(act):
                for c, (w, b) in enumerate(((0, 0), (1, 0), (1, 1))):
                    for k, ws in enumerate(((Wq0, Wq1), (Wk0, Wk1), (Wv0, Wv1))):
                        act.dma_start(wa_f[:, c, k, :], ws[w][b * P:(b + 1) * P, :]).then_inc(wa_in, 16)
                act.dma_start(wo_f[:, :, :], Wout.rearrange("(c p) d -> p c d", p=P)).then_inc(wa_in, 16)
                for r, b in enumerate((bq0, bq1, bk0, bk1, bv0, bv1)):
                    act.dma_start(brows[r:r + 1, :], b.rearrange("(a d) -> a d", a=1)).then_inc(row_in, 16)
                act.dma_start(brows[6:6 + NB1, :], b1.rearrange("e (c p) -> (e c) p", p=P)).then_inc(row_in, 16)
                act.dma_start(bout_bc[:, :], bout.rearrange("(a d) -> a d", a=1).broadcast_to([P, D])).then_inc(wf_in, 16)
                act.dma_start(bg_bc[:, :], bg.rearrange("(a d) -> a d", a=1).broadcast_to([P, E])).then_inc(wf_in, 16)
                act.dma_start(wg_f[:, :], Wg).then_inc(ffn_in, 16)
                act.dma_start(b2_f[:, :], b2).then_inc(ffn_in, 16)
                act.dma_start(w1_f[:, :, :], W1.rearrange("e d h -> d e h")).then_inc(ffn_in, 16)
                act.dma_start(w2_f[:, :, :, :], W2.rearrange("e (c p) d -> p e c d", p=P)).then_inc(ffn_in, 16)
                act.wait_ge(var_set[0], 1)
                nc.scalar.activation(rstd[0][:, :], sa[:, :], ACT.Sqrt, bias=eps_c[:, 0:1]).then_inc(std_set[0], 1)
                act.wait_ge(ffn_in, 64)
                nc.scalar.activation(w1_hi[:, :, :], w1_f[:, :, :], ACT.Copy).then_inc(ffn_hi_set, 1)
                nc.scalar.activation(w2_hi[:, :, :, :], w2_f[:, :, :, :], ACT.Copy).then_inc(ffn_hi_set, 1)
                nc.scalar.activation(wg_hi[:, :], wg_f[:, :], ACT.Copy).then_inc(ffn_hi_set, 1)
                nc.scalar.activation(b2_hi[:, :], b2_f[:, :], ACT.Copy).then_inc(ffn_hi_set, 1)
                act.wait_ge(b_ready, 1)

                def turned_hi(l, i):
                    for j in range(2):
                        act.wait_ge(T_fill[j], n(OT, "BC"[l], i) + 1)
                        nc.scalar.activation(prT_hi[l][:, j, :, :].rearrange("p a b -> p (a b)"), bT[j][:, :],
                                             ACT.Copy).then_inc(T_hi[j], 1)

                def rows_hi(dst, bias, stage, i):
                    act.wait_ge(X_fill, n(OX, stage, i) + 1)
                    if bias is None:
                        if not isinstance(i, int) or i >= 2:
                            act.wait_ge(xT_kept, i - 1)
                        nc.scalar.activation(dst[:, 0, :], bX[:, 0:TOK], ACT.Copy).then_inc(X_hi, 1)
                    else:
                        nc.scalar.activation(dst[:, 0, :], bX[:, 0:TOK], ACT.Identity, bias=bias).then_inc(X_hi, 1)

                def qkv_hi(l, i):
                    act.wait_ge(Q_fill, n(OQ, "AB"[l], i) + 1)
                    nc.scalar.activation(qT[l][:, 0, :], bQ[:, 0:TOK], ACT.Identity, bias=bq[l])
                    nc.scalar.activation(kT[l][:, 0, :], bQ[:, TOK:2 * TOK], ACT.Identity, bias=bk[l]).then_inc(Q_hi, 1)
                    act.wait_ge(V_fill, n(OV, "AB"[l], i) + 1)
                    nc.scalar.activation(v_hi[l][:, :, :, 0:HD].rearrange("p u h d -> p (u h) d"),
                                         bV[:, 0:TOK].rearrange("p (a d) -> p a d", d=HD), ACT.Copy).then_inc(V_hi, 1)

                def exps(l, i):
                    for j in range(2):
                        act.wait_ge(S_max[j], n(OS, "AB"[l], i) + 1)
                        for a in range(2 * U):
                            last = nc.scalar.activation(pr[l][:, j, a, :], bS[j][:, a * T:(a + 1) * T], ACT.Exp,
                                                        bias=nmax[:, l, j, a:a + 1])
                        last.then_inc(S_empty[j], 1)

                def act_step(i, p):
                    if active("B", i):
                        turned_hi(0, i)
                    if active("C", i):
                        turned_hi(1, i)
                    if active("A", i):
                        rows_hi(xT[p], None, "A", i)
                        qkv_hi(0, i)
                    if active("B", i):
                        rows_hi(h0T[1 - p], bv[0], "B", i)
                    if active("C", i):
                        rows_hi(h1T, bv[1], "C", i)
                    if active("A", i):
                        exps(0, i)
                    if active("B", i):
                        qkv_hi(1, i)
                        exps(1, i)

                steps(act, act_step)
                act.wait_ge(var_set[1], 1)
                nc.scalar.activation(rstd[1][:, :], sa[:, :], ACT.Sqrt, bias=eps_c[:, 0:1]).then_inc(std_set[1], 1)

            @block.vector
            def _(dve):
                done = [0]

                def then_wait(ins):
                    done[0] += 1
                    ins.then_inc(prep, 1)
                    dve.wait_ge(prep, done[0])

                def layer_norm_scalars(k):
                    s = st[k]
                    nc.vector.tensor_tensor(sa[:, :], s[:, :, 1], s[:, :, 4], ALU.subtract)
                    then_wait(nc.vector.tensor_tensor(nmr[k][:, :], s[:, :, 1], s[:, :, 4], ALU.add))
                    then_wait(nc.vector.scalar_tensor_tensor(out=sbb[:, :], in0=sa[:, :], scalar=0.25, in1=sa[:, :],
                                                             op0=ALU.mult, op1=ALU.mult))
                    then_wait(nc.vector.scalar_tensor_tensor(out=sbb[:, :], in0=s[:, :, 2], scalar=1.0 / D, in1=sbb[:, :],
                                                             op0=ALU.mult, op1=ALU.add))
                    nc.vector.scalar_tensor_tensor(out=sa[:, :], in0=s[:, :, 5], scalar=1.0 / D, in1=sbb[:, :],
                                                   op0=ALU.mult, op1=ALU.add).then_inc(var_set[k], 1)
                    dve.wait_ge(std_set[k], 1)
                    then_wait(nc.vector.reciprocal(rstd[k][:, :], rstd[k][:, :]))
                    nc.vector.scalar_tensor_tensor(out=nmr[k][:, :], in0=nmr[k][:, :], scalar=-0.5, in1=rstd[k][:, :],
                                                   op0=ALU.mult, op1=ALU.mult).then_inc(ln_ready[k], 1)

                nc.vector.memset(eps_c[:, :], EPS)
                nc.vector.memset(held_v[:, :], 0.0)
                for l in range(2):
                    nc.vector.memset(v_hi[l][:, :, :, HD:HD + 1], 1.0)
                scale = float(HD) ** -0.5
                dve.wait_ge(wa_in, 160)
                for c in range(3):
                    then_wait(nc.vector.tensor_scalar(wa_f[:, c, 0, :], wa_f[:, c, 0, :], scale, None, ALU.mult))
                nc.vector.tensor_copy(wo_hi[:, :, :], wo_f[:, :, :])
                then_wait(nc.vector.tensor_copy(wa_hi[:, :, :, :], wa_f[:, :, :, :]))
                nc.vector.tensor_tensor(wo_lo[:, :, :], wo_f[:, :, :], wo_hi[:, :, :], ALU.subtract)
                then_wait(nc.vector.tensor_tensor(wa_lo[:, :, :, :].rearrange("p a b c -> p (a b c)"),
                                                  wa_f[:, :, :, :].rearrange("p a b c -> p (a b c)"),
                                                  wa_hi[:, :, :, :].rearrange("p a b c -> p (a b c)"), ALU.subtract))
                dve.wait_ge(b_turned, 1)
                then_wait(nc.vector.tensor_copy(bcols[:, :], bX[:, 0:6 + NB1]))
                nc.vector.tensor_scalar(bcols[:, 0:2], bcols[:, 0:2], scale, None, ALU.mult).then_inc(b_ready, 1)
                per = B // XCH
                for b in range(B):
                    if b % per == 0:
                        dve.wait_ge(x_in[b // per], 16)
                    last = nc.vector.bn_stats(st[0][:, b, :], xs[:, b, :])
                then_wait(last)
                layer_norm_scalars(0)
                dve.wait_ge(wf_in, 32)
                dve.wait_ge(b_ready, 1)

                def turned_lo(l, i):
                    for j in range(2):
                        dve.wait_ge(T_hi[j], n(OT, "BC"[l], i) + 1)
                        nc.vector.tensor_tensor(prT_lo[l][:, j, :, :].rearrange("p a b -> p (a b)"), bT[j][:, :],
                                                prT_hi[l][:, j, :, :].rearrange("p a b -> p (a b)"),
                                                ALU.subtract).then_inc(T_empty[j], 1)

                def rows_lo(dst, bias, stage, i):
                    dve.wait_ge(X_hi, n(OX, stage, i) + 1)
                    if bias is None:
                        nc.vector.tensor_tensor(dst[:, 1, :], bX[:, 0:TOK], dst[:, 0, :],
                                                ALU.subtract).then_inc(X_empty, 1)
                    else:
                        nc.vector.scalar_tensor_tensor(out=dst[:, 1, :], in0=bX[:, 0:TOK], scalar=bias,
                                                       in1=dst[:, 0, :], op0=ALU.add,
                                                       op1=ALU.subtract).then_inc(X_empty, 1)

                def qkv_lo(l, i):
                    dve.wait_ge(Q_hi, n(OQ, "AB"[l], i) + 1)
                    nc.vector.scalar_tensor_tensor(out=qT[l][:, 1, :], in0=bQ[:, 0:TOK], scalar=bq[l],
                                                   in1=qT[l][:, 0, :], op0=ALU.add, op1=ALU.subtract)
                    nc.vector.scalar_tensor_tensor(out=kT[l][:, 1, :], in0=bQ[:, TOK:2 * TOK], scalar=bk[l],
                                                   in1=kT[l][:, 0, :], op0=ALU.add,
                                                   op1=ALU.subtract).then_inc(Q_empty, 1)
                    dve.wait_ge(V_hi, n("AB", "AB"[l], i) + 1)
                    nc.vector.tensor_tensor(v_lo[l][:, :, :, :].rearrange("p u h d -> p (u h) d"),
                                            bV[:, 0:TOK].rearrange("p (a d) -> p a d", d=HD),
                                            v_hi[l][:, :, :, 0:HD].rearrange("p u h d -> p (u h) d"),
                                            ALU.subtract).then_inc(V_empty, 1)

                def maxima(l, i):
                    for j in range(2):
                        dve.wait_ge(S_fill[j], n(OS, "AB"[l], i) + 1)
                        nc.vector.tensor_reduce(nmax[:, l, j, :], bS[j][:, :].rearrange("p (a k) -> p a k", k=T),
                                                axis=AX.X, op=ALU.max, negate=True).then_inc(S_max[j], 1)

                def normalise(l, i):
                    o = bO[:, 0:U * HEADS * (HD + 1)].rearrange("p (a d) -> p a d", d=HD + 1)
                    dve.wait_ge(O_fill, n(OO, "BC"[l], i) + 1)
                    nc.vector.reciprocal(rden[:, l, :], o[:, :, HD]).then_inc(O_rden, 1)
                    dve.wait_ge(O_rden, n(OO, "BC"[l], i) + 1)
                    nc.vector.tensor_tensor(hn[l][:, :, :].rearrange("p u (h d) -> p (u h) d", d=HD), o[:, :, 0:HD],
                                            rden[:, l, :].unsqueeze(2).broadcast_to([P, U * HEADS, HD]),
                                            ALU.mult).then_inc(O_empty, 1)

                def residual(i):
                    dve.wait_ge(V_fill, n(OV, "C", i) + 1)
                    nc.vector.tensor_tensor(og[:, :, :], bV[:, 0:TOK].rearrange("p (u d) -> p u d", u=U),
                                            bout_bc[:, :].unsqueeze(1).broadcast_to([P, U, D]),
                                            ALU.add).then_inc(V_empty, 1)
                    dve.wait_ge(V_empty, n(OV, "C", i) + 1)
                    sl = bass.ds((i - 2) * U, U)
                    nc.vector.scalar_tensor_tensor(out=xs[:, sl, :].rearrange("p u d -> p (u d)"), in0=og[:, :, :].rearrange("p u d -> p (u d)"), scalar=0.0, in1=xs[:, sl, :].rearrange("p u d -> p (u d)"),
                                                   op0=ALU.max, op1=ALU.add).then_inc(x2_set, 1)
                    dve.wait_ge(x2_set, i - 1)
                    for u in range(U):
                        b = (i - 2) * U + u
                        nc.vector.bn_stats(st[1][:, bass.ds(b, 1), :].rearrange("p a s -> p (a s)"),
                                           xs[:, bass.ds(b, 1), :].rearrange("p a d -> p (a d)")).then_inc(st_set, 1)

                def dve_step(i, p):
                    if active("B", i):
                        turned_lo(0, i)
                    if active("C", i):
                        turned_lo(1, i)
                    if active("A", i):
                        rows_lo(xT[p], None, "A", i)
                    if active("B", i):
                        normalise(0, i)
                    if active("C", i):
                        normalise(1, i)
                    if active("A", i):
                        qkv_lo(0, i)
                    if active("B", i):
                        rows_lo(h0T[1 - p], bv[0], "B", i)
                    if active("C", i):
                        rows_lo(h1T, bv[1], "C", i)
                    if active("A", i):
                        maxima(0, i)
                    if active("B", i):
                        qkv_lo(1, i)
                    if active("C", i):
                        residual(i)
                    if active("B", i):
                        maxima(1, i)

                steps(dve, dve_step)
                dve.wait_ge(st_set, B)
                layer_norm_scalars(1)

            @block.tensor
            def _(pe):
                pe.wait_ge(row_in, 112)
                pe.wait_ge(ident_set, 4)
                nc.tensor.transpose(bX[:, 0:6 + NB1], brows[:, :], ident[0:6 + NB1, 0:6 + NB1]).then_inc(b_turned, 1)
                pe.wait_ge(b_ready, 1)

                def turn_rows(src, order_sem, value, stage, i):
                    pe.wait_ge(order_sem, value)
                    if not isinstance(i, int) or n(OX, stage, i):
                        pe.wait_ge(X_empty, n(OX, stage, i))
                    for u in range(U):
                        last = nc.tensor.transpose(bX[:, u * T:(u + 1) * T], src[:, u, :], ident[:, :])
                    last.then_inc(X_fill, 1)

                def project(l, rows, ready, i):
                    pe.wait_ge(X_empty, ready)
                    if not isinstance(i, int) or n(OQ, "AB"[l], i):
                        pe.wait_ge(Q_empty, n(OQ, "AB"[l], i))
                    for k in range(2):
                        last = summed(bQ[:, k * TOK:(k + 1) * TOK],
                                      [((wa_hi[:, c, k, :], wa_lo[:, c, k, :]), (r[:, 0, :], r[:, 1, :])) for c, r in rows])
                    last.then_inc(Q_fill, 1)
                    if not isinstance(i, int) or n(OV, "AB"[l], i):
                        pe.wait_ge(V_empty, n(OV, "AB"[l], i))
                    for u in range(U):
                        ts = slice(u * T, (u + 1) * T)
                        last = summed(bV[:, ts], [((r[:, 0, ts], r[:, 1, ts]), (wa_hi[:, c, 2, :], wa_lo[:, c, 2, :]))
                                                  for c, r in rows])
                    last.then_inc(V_fill, 1)

                def score(l, i, p):
                    stage = "AB"[l]
                    if l == 0:
                        pe.wait_ge(mask_set, i + 1)
                    pe.wait_ge(Q_empty, n(OQ, stage, i) + 1)
                    for j in range(2):
                        if not isinstance(i, int) or n(OS, stage, i):
                            pe.wait_ge(S_empty[j], n(OS, stage, i))
                    for h in range(HEADS):
                        j, w = h % 2, h // 2
                        cols = slice(w * U * T, (w + 1) * U * T)
                        if w:
                            pe.wait_ge(half_done[j], n(OS, stage, i) + 1)
                        nc.tensor.matmul(bS[j][:, cols], ident_b[:, :],
                                         mask_b[p][:, :, :].rearrange("p u k -> p (u k)"), start=w == 0, stop=False)
                        hs = slice(h * HD, (h + 1) * HD)
                        for u in range(U):
                            ts = slice(u * T, (u + 1) * T)
                            a = w * U + u
                            for m, (qh, kh) in enumerate(((0, 0), (0, 1), (1, 0))):
                                last = nc.tensor.matmul(bS[j][:, a * T:(a + 1) * T], qT[l][hs, qh, ts],
                                                        kT[l][hs, kh, ts], start=False,
                                                        stop=m == 2 and a == 2 * U - 1)
                        last.then_inc(S_fill[j] if w else half_done[j], 1)

                def turn_probs(l, i):
                    stage = "BC"[l]
                    for j in range(2):
                        pe.wait_ge(S_empty[j], n(OS, "AB"[l], i - 1) + 1)
                        if not isinstance(i, int) or n(OT, stage, i):
                            pe.wait_ge(T_empty[j], n(OT, stage, i))
                        for a in range(2 * U):
                            last = nc.tensor.transpose(bT[j][:, a * T:(a + 1) * T], pr[l][:, j, a, :], ident[:, :])
                        last.then_inc(T_fill[j], 1)

                def weigh(l, i):
                    stage = "BC"[l]
                    if not isinstance(i, int) or n(OO, stage, i):
                        pe.wait_ge(O_empty, n(OO, stage, i))
                    pe.wait_ge(V_empty, n(OV, "AB"[l], i - 1) + 1)
                    for j in range(2):
                        pe.wait_ge(T_empty[j], n(OT, stage, i) + 1)
                    for u in range(U):
                        for h in range(HEADS):
                            j, a = h % 2, U * (h // 2) + u
                            o = (u * HEADS + h) * (HD + 1)
                            nc.tensor.matmul(bO[:, o:o + HD + 1], prT_hi[l][:, j, a, :], v_hi[l][:, u, h, :],
                                             start=True, stop=False)
                            nc.tensor.matmul(bO[:, o:o + HD], prT_hi[l][:, j, a, :], v_lo[l][:, u, h, :],
                                             start=False, stop=False, skip_group_check=True)
                            last = nc.tensor.matmul(bO[:, o:o + HD + 1], prT_lo[l][:, j, a, :], v_hi[l][:, u, h, :],
                                                    start=False, stop=True)
                    last.then_inc(O_fill, 1)

                def output(i, p):
                    pe.wait_ge(X_empty, n(OX, "C", i) + 1)
                    pe.wait_ge(xT_kept, i - 1)
                    if not isinstance(i, int) or n(OV, "C", i):
                        pe.wait_ge(V_empty, n(OV, "C", i))
                    for u in range(U):
                        ts = slice(u * T, (u + 1) * T)
                        last = summed(bV[:, ts], [((r[:, 0, ts], r[:, 1, ts]), (wo_hi[:, c, :], wo_lo[:, c, :]))
                                                  for c, r in enumerate((xTk[p], h0T[p], h1T))])
                    last.then_inc(V_fill, 1)

                def pe_step(i, p):
                    if active("B", i):
                        turn_probs(0, i)
                    if active("C", i):
                        turn_probs(1, i)
                    if active("A", i):
                        turn_rows(xn[p], xn_set, i + 1, "A", i)
                    if active("B", i):
                        weigh(0, i)
                    if active("C", i):
                        weigh(1, i)
                    if active("A", i):
                        project(0, [(0, xT[p])], n(OX, "A", i) + 1, i)
                    if active("B", i):
                        turn_rows(hn[0], O_empty, n(OO, "B", i) + 1, "B", i)
                    if active("C", i):
                        turn_rows(hn[1], O_empty, n(OO, "C", i) + 1, "C", i)
                    if active("A", i):
                        score(0, i, p)
                    if active("B", i):
                        project(1, [(1, xT[1 - p]), (2, h0T[1 - p])], n(OX, "B", i) + 1, i)
                    if active("C", i):
                        output(i, p)
                    if active("B", i):
                        score(1, i, 1 - p)

                steps(pe, pe_step)

        bH = [[bQ, bV], [bO, bX]]
        bY = bS
        bR, bG = bT
        xr_mul, xr_set = sem("xr_mul"), sem("xr_set")
        R_fill, R_hi, R_empty = sem("R_fill"), sem("R_hi"), sem("R_empty")
        G_fill, G_empty = sem("G_fill"), sem("G_empty")
        chain = sem("chain")
        mk_set = sem("mk_set")
        H_fill, H_gelu, H_hi, H_lo = sem("H_fill"), sem("H_gelu"), sem("H_hi"), sem("H_lo")
        Y_fill, Y_empty = sem("Y_fill"), sem("Y_empty")
        acc_set, acc_init = sem("acc_set"), sem("acc_init")

        def groups(eng, body):
            body(-1, 1)
            body(0, 0)
            body(1, 1)
            with eng.Fori(2, GROUPS - 3, 2) as g:
                body(g, 0)
                body(g + 1, 1)
            body(GROUPS - 2, 0)
            body(GROUPS - 1, 1)

        def has(g):
            return not isinstance(g, int) or g >= 0

        def has_next(g):
            return not isinstance(g, int) or g + 1 < GROUPS

        TURN, GATE, MASKT, BIAS2 = 0, 2, 4, 6

        with nc.Block() as block:

            @block.gpsimd
            def _(pool):
                def body(g, p):
                    if has_next(g):
                        sl = bass.ds((g + 1) * G, G)
                        if has(g):
                            pool.wait_ge(R_fill, 2 * g + 1)
                        nc.gpsimd.tensor_tensor(xn2[:, :, :], xs[:, sl, :],
                                                rstd[1][:, sl].unsqueeze(2).broadcast_to([P, G, D]),
                                                ALU.mult).then_inc(xr_mul, 1)
                        pool.wait_ge(xr_mul, g + 2)
                        nc.gpsimd.tensor_tensor(xn2[:, :, :], xn2[:, :, :],
                                                nmr[1][:, sl].unsqueeze(2).broadcast_to([P, G, D]),
                                                ALU.add).then_inc(xr_set, 1)

                groups(pool, body)

            @block.sync
            def _(sp):
                def body(g, p):
                    if has(g):
                        sp.wait_ge(acc_set, (g + 1) * E)
                        sp.dma_start(out[bass.ds(g * G, G)].rearrange("b t d -> t b d"),
                                     acc[p][:, :, :]).then_inc(out_done[p], 16)

                groups(sp, body)
                for p in range(2):
                    sp.wait_ge(out_done[p], 16 * (GROUPS // 2))

            @block.scalar
            def _(act):
                def body(g, p):
                    for e in range(E):
                        if e == TURN and has_next(g):
                            act.wait_ge(R_fill, 2 * (g + 1) + 1)
                            nc.scalar.activation(x2T[1 - p][:, 0, :], bR[:, :], ACT.Copy).then_inc(R_hi, 1)
                        if has(g):
                            q = e % 2
                            ge = g * E + e
                            act.wait_ge(H_fill, ge + 1)
                            if not isinstance(g, int) or g > 0 or e >= 2:
                                act.wait_ge(H_lo, ge - 1)
                            for c in range(NC):
                                col = 6 + e * NC + c
                                last = nc.scalar.activation(hg[q][:, c, :], bH[q][c][:, :], ACT.Gelu,
                                                            bias=bcols[:, col:col + 1])
                            last.then_inc(H_gelu, 1)
                            act.wait_ge(H_gelu, ge + 1)
                            if not isinstance(g, int) or g > 0 or e >= 2:
                                act.wait_ge(Y_fill, ge - 1)
                            nc.scalar.activation(hg_hi[q][:, :, :], hg[q][:, :, :], ACT.Copy).then_inc(H_hi, 1)

                groups(act, body)

            @block.vector
            def _(dve):
                STEPS = 4

                def body(g, p):
                    for e in range(E):
                        if has_next(g):
                            step = [STEPS * (g + 1)]

                            def then_wait(ins):
                                ins.then_inc(chain, 1)
                                step[0] = step[0] + 1
                                dve.wait_ge(chain, step[0])

                            if e == TURN:
                                dve.wait_ge(R_hi, g + 2)
                                nc.vector.tensor_tensor(x2T[1 - p][:, 1, :], bR[:, :], x2T[1 - p][:, 0, :],
                                                        ALU.subtract).then_inc(R_empty, 1)
                            if e == GATE:
                                dve.wait_ge(G_fill, 2 * (g + 1) + 1)
                                nc.vector.tensor_tensor(gs[:, :, :], bG[:, 0:G * E].rearrange("p (b e) -> p b e", e=E),
                                                        bg_bc[:, :].unsqueeze(1).broadcast_to([P, G, E]),
                                                        ALU.add).then_inc(G_empty, 1)
                                dve.wait_ge(G_empty, 2 * (g + 1) + 1)
                                hold(nc.vector, held_v)
                                for b in range(G):
                                    last = nc.vector.max(top[:, b, :], gs[:, b, :])
                                then_wait(last)
                                hold(nc.vector, held_v)
                                for b in range(G):
                                    last = nc.vector.max_index(topi[:, b, :], top[:, b, :], gs[:, b, :])
                                then_wait(last)
                                then_wait(nc.vector.tensor_copy(topf[:, :, :], topi[:, :, 0:2]))
                                for k in range(2):
                                    last = nc.vector.tensor_tensor(eq[:, k, :, :],
                                                                   iota8[:, :].unsqueeze(1).broadcast_to([P, G, E]),
                                                                   topf[:, :, k:k + 1].broadcast_to([P, G, E]), ALU.is_equal)
                                then_wait(last)
                                nc.vector.tensor_tensor(mk[1 - p][:, :, :], eq[:, 0, :, :], eq[:, 1, :, :],
                                                        ALU.add).then_inc(mk_set, 1)
                            if e == MASKT:
                                dve.wait_ge(G_fill, 2 * (g + 1) + 2)
                                nc.vector.tensor_copy(mkT[:, :], bG[0:E, :]).then_inc(G_empty, 1)
                            if e == BIAS2:
                                dve.wait_ge(R_fill, 2 * (g + 1) + 2)
                                if has(g) and (not isinstance(g, int) or g > 0):
                                    dve.wait_ge(out_done[1 - p], 8 * g + 8 * p)
                                nc.vector.tensor_tensor(acc[1 - p][:, :, :], bR[:, :].rearrange("p (b d) -> p b d", d=D),
                                                        xs[:, bass.ds((g + 1) * G, G), :], ALU.add).then_inc(R_empty, 1)
                        if has(g):
                            q = e % 2
                            ge = g * E + e
                            dve.wait_ge(H_hi, ge + 1)
                            nc.vector.tensor_tensor(hg_lo[q][:, :, :].rearrange("p c t -> p (c t)"),
                                                    hg[q][:, :, :].rearrange("p c t -> p (c t)"),
                                                    hg_hi[q][:, :, :].rearrange("p c t -> p (c t)"), ALU.subtract).then_inc(H_lo, 1)
                            if e > 0:
                                masked_add(g, p, e - 1)
                    if has(g):
                        masked_add(g, p, E - 1)

                def masked_add(g, p, e):
                    q = e % 2
                    ge = g * E + e
                    dve.wait_ge(Y_fill, ge + 1)
                    nc.vector.tensor_tensor(ym[q][:, :, :], bY[q][:, :].rearrange("p (b d) -> p b d", d=D),
                                            mk[p][:, :, e:e + 1].broadcast_to([P, G, D]), ALU.mult).then_inc(Y_empty, 1)
                    dve.wait_ge(Y_empty, ge + 1)
                    if e == 0:
                        dve.wait_ge(R_empty, 2 * g + 2)
                    else:
                        dve.wait_ge(acc_set, ge)
                    nc.vector.tensor_tensor(acc[p][:, :, :], acc[p][:, :, :], ym[q][:, :, :],
                                            ALU.add).then_inc(acc_set, 1)

                groups(dve, body)

            @block.tensor
            def _(pe):
                def first(g, p, e):
                    q = e % 2
                    ge = g * E + e
                    if e == 0:
                        pe.wait_ge(R_empty, 2 * g + 1)
                    if not isinstance(g, int) or g > 0 or e >= 2:
                        pe.wait_ge(H_gelu, ge - 1)
                    for c in range(NC):
                        cs = slice(c * P, (c + 1) * P)
                        last = summed(bH[q][c][:, :], [((w1_hi[:, e, cs], w1_lo[:, e, cs]),
                                                        (x2T[p][:, 0, :], x2T[p][:, 1, :]))])
                    last.then_inc(H_fill, 1)

                def second(g, p, e):
                    q = e % 2
                    ge = g * E + e
                    pe.wait_ge(H_lo, ge + 1)
                    if not isinstance(g, int) or g > 0 or e >= 2:
                        pe.wait_ge(Y_empty, ge - 1)
                    for b in range(G):
                        ts = slice(b * T, (b + 1) * T)
                        last = summed(bY[q][:, ts], [((hg_hi[q][:, c, ts], hg_lo[q][:, c, ts]),
                                                      (w2_hi[:, e, c, :], w2_lo[:, e, c, :])) for c in range(NC)])
                    last.then_inc(Y_fill, 1)

                def body(g, p):
                    for e in range(E):
                        if has_next(g):
                            m = 2 * (g + 1)
                            if e == TURN:
                                pe.wait_ge(xr_set, g + 2)
                                if has(g):
                                    pe.wait_ge(R_empty, m)
                                for b in range(G):
                                    last = nc.tensor.transpose(bR[:, b * T:(b + 1) * T], xn2[:, b, :], ident[:, :])
                                last.then_inc(R_fill, 1)
                            if e == GATE:
                                pe.wait_ge(R_empty, m + 1)
                                if has(g):
                                    pe.wait_ge(G_empty, m)
                                for b in range(G):
                                    ts = slice(b * T, (b + 1) * T)
                                    last = summed(bG[:, b * E:(b + 1) * E],
                                                  [((x2T[1 - p][:, 0, ts], x2T[1 - p][:, 1, ts]), (wg_hi[:, :], wg_lo[:, :]))])
                                last.then_inc(G_fill, 1)
                            if e == MASKT:
                                pe.wait_ge(mk_set, g + 2)
                                pe.wait_ge(G_empty, m + 1)
                                for b in range(G):
                                    last = nc.tensor.transpose(bG[0:E, b * T:(b + 1) * T], mk[1 - p][:, b, :], ident[:, :])
                                last.then_inc(G_fill, 1)
                            if e == BIAS2:
                                pe.wait_ge(G_empty, m + 2)
                                for b in range(G):
                                    ts = slice(b * T, (b + 1) * T)
                                    nc.tensor.matmul(bR[:, ts], mkT[:, ts], b2_hi[:, :], start=True, stop=False)
                                    last = nc.tensor.matmul(bR[:, ts], mkT[:, ts], b2_lo[:, :], start=False, stop=True)
                                last.then_inc(R_fill, 1)
                        if has(g):
                            if e + 1 < E:
                                first(g, p, e + 1)
                            elif has_next(g):
                                first(g + 1, 1 - p, 0)
                            second(g, p, e)
                    if not has(g):
                        first(0, 0, 0)

                groups(pe, body)


_INS = ["x", "adj", "L0_gnn_Wq0", "L0_gnn_bq0", "L0_gnn_Wk0", "L0_gnn_bk0", "L0_gnn_Wv0", "L0_gnn_bv0",
        "L0_gnn_Wq1", "L0_gnn_bq1", "L0_gnn_Wk1", "L0_gnn_bk1", "L0_gnn_Wv1", "L0_gnn_bv1",
        "L0_gnn_Wout", "L0_gnn_bout", "L0_ffn_Wg", "L0_ffn_bg", "L0_ffn_W1", "L0_ffn_b1", "L0_ffn_W2", "L0_ffn_b2"]


def kernel(**inputs):
    import numpy as np
    import concourse.bacc as bacc
    from concourse.bass_utils import run_bass_kernel_spmd

    nc = bacc.Bacc("TRN2", target_bir_lowering=False, num_devices=1)
    arrays, args = {}, []
    for name in _INS:
        a = np.ascontiguousarray(inputs[name])
        arrays[f"in_{name}"] = a
        args.append(nc.dram_tensor(f"in_{name}", a.shape, mybir.dt.from_np(a.dtype), kind="ExternalInput").ap())
    args.append(nc.dram_tensor("out", inputs["x"].shape, F32, kind="ExternalOutput").ap())
    gnn_moe_kernel(nc, *args)
    r = run_bass_kernel_spmd(nc, [arrays], core_ids=[0])
    return r.results[0]["out"]
```

```python
from contextlib import ExitStack

import concourse.bass as bass
from concourse import mybir

F32 = mybir.dt.float32
F16 = mybir.dt.float16
BF16 = mybir.dt.bfloat16
I32 = mybir.dt.int32
U32 = mybir.dt.uint32
ALU = mybir.AluOpType
ACT = mybir.ActivationFunctionType
AX = mybir.AxisListType

P = 128
HEADS = 4
EPS = 1e-5
MASKED = -(2.0 ** 100)

ORDER = (("output", 3), ("probs0", 1), ("rows_x", 0), ("sums0", 1), ("qkv0", 0), ("probs1", 2),
         ("rows_h0", 1), ("scores0", 0), ("sums1", 2), ("qkv1", 1), ("rows_h1", 2), ("scores1", 1))
LAG = dict(ORDER)
LAST = max(LAG.values())
BANKS = {"X": ("rows_x", "rows_h0", "rows_h1"), "Q": ("qkv0", "qkv1"), "V": ("qkv0", "qkv1", "output"),
         "O": ("sums0", "sums1"), "S": ("scores0", "scores1"), "T": ("probs0", "probs1"), "VH": ("qkv0", "qkv1")}


def uses(bank, work, u, units):
    order = [w for w, _ in ORDER if w in BANKS[bank]]
    i = u + LAG[work]
    before = order.index(work)
    if not isinstance(u, int):
        return i * len(order) - sum(LAG[w] for w in order) + before
    done = sum(min(max(i - LAG[w], 0), units) for w in order)
    return done + sum(0 <= i - LAG[w] < units for w in order[:before])


def gnn_moe_kernel(nc, x, adj, Wq0, bq0, Wk0, bk0, Wv0, bv0, Wq1, bq1, Wk1, bk1, Wv1, bv1,
                   Wout, bout, Wg, bg, W1, b1, W2, b2, out):
    B, T, D = x.shape
    E, _, HID = W1.shape
    assert T == P and D == P and HID == 2 * P and B % 8 == 0
    HD = D // HEADS
    U = 2
    UNITS = B // U
    TOK = U * T
    NC = HID // P
    NB1 = E * NC
    G = 4
    GROUPS = B // G
    GT = G * T
    XCH = 8
    HEAD = 2 * LAST
    assert UNITS % 2 == 0 and HEAD < UNITS

    with ExitStack() as ctx:
        def sb(name, shape, dt=F32):
            return ctx.enter_context(nc.sbuf_tensor(name, shape, dt))

        def pb(name, shape=(P, 512), dt=F32):
            return ctx.enter_context(nc.psum_tensor(name, list(shape), dt))

        def sem(name):
            return ctx.enter_context(nc.semaphore(name))

        ident = sb("ident", [P, P])
        ident_b = sb("ident_b", [P, P], BF16)
        iota8 = sb("iota8", [P, E])
        brows = sb("brows", [6 + NB1, P])
        bcols = sb("bcols", [P, 6 + NB1])
        bq = [bcols[:, 0:1], bcols[:, 1:2]]
        bk = [bcols[:, 2:3], bcols[:, 3:4]]
        bv = [bcols[:, 4:5], bcols[:, 5:6]]
        bout_bc = sb("bout_bc", [P, D])
        bg_bc = sb("bg_bc", [P, E])
        b2_f = sb("b2_f", [E, D])
        b2_hi = sb("b2_hi", [E, D], F16)
        b2_lo = sb("b2_lo", [E, D], BF16)
        wa_f = sb("wa_f", [P, 3, 3, D])
        wa_hi = sb("wa_hi", [P, 3, 3, D], F16)
        wa_lo = sb("wa_lo", [P, 3, 3, D], BF16)
        wo_f = sb("wo_f", [P, 3, D])
        wo_hi = sb("wo_hi", [P, 3, D], F16)
        wo_lo = sb("wo_lo", [P, 3, D], BF16)
        wg_f = sb("wg_f", [P, E])
        wg_hi = sb("wg_hi", [P, E], F16)
        wg_lo = sb("wg_lo", [P, E], BF16)
        w1_f = sb("w1_f", [P, E, HID])
        w1_hi = sb("w1_hi", [P, E, HID], F16)
        w1_lo = sb("w1_lo", [P, E, HID], BF16)
        w2_f = sb("w2_f", [P, E, NC, D])
        w2_hi = sb("w2_hi", [P, E, NC, D], F16)
        w2_lo = sb("w2_lo", [P, E, NC, D], BF16)

        held_p = sb("held_p", [P, 2])
        held_v = sb("held_v", [P, 2])

        xs = sb("xs", [P, B, D])
        st = [sb("st0", [P, B, 6]), sb("st1", [P, B, 6])]
        rstd = [sb("rstd0", [P, B]), sb("rstd1", [P, B])]
        nmr = [sb("nmr0", [P, B]), sb("nmr1", [P, B])]
        sa = sb("sa", [P, B])
        sbb = sb("sbb", [P, B])
        eps_c = sb("eps_c", [P, 1])

        adj_t = [sb(f"adj{p}", [P, U, T], I32) for p in range(2)]
        mask_b = [sb(f"mask{p}", [P, U, T], BF16) for p in range(2)]
        xn = [sb(f"xn{p}", [P, U, D]) for p in range(2)]
        xT = [sb(f"xT{p}", [P, 2, TOK], F16) for p in range(2)]
        xTk = [sb(f"xTk{p}", [P, 2, TOK], F16) for p in range(2)]
        h0T = [sb(f"h0T{p}", [P, 2, TOK], F16) for p in range(2)]
        h1T = sb("h1T", [P, 2, TOK], F16)
        qT = [sb(f"qT{l}", [P, 2, TOK], F16) for l in range(2)]
        kT = [sb(f"kT{l}", [P, 2, TOK], F16) for l in range(2)]
        v_hi = [sb(f"v_hi{l}", [P, U, HEADS, HD + 1], F16) for l in range(2)]
        v_lo = [sb(f"v_lo{l}", [P, U, HEADS, HD], F16) for l in range(2)]
        pr = [sb(f"pr{l}", [P, 2, 2 * U, T]) for l in range(2)]
        prT_hi = [sb(f"prT_hi{l}", [P, 2, 2 * U, T], F16) for l in range(2)]
        prT_lo = [sb(f"prT_lo{l}", [P, 2, 2 * U, T], F16) for l in range(2)]
        nmax = sb("nmax", [P, 2, 2, 2 * U])
        rden = sb("rden", [P, 2, U * HEADS])
        hn = [sb(f"hn{l}", [P, U, D]) for l in range(2)]
        og = sb("og", [P, U, D])

        xn2 = sb("xn2", [P, G, D])
        x2T = [sb(f"x2T{p}", [P, 2, GT], F16) for p in range(2)]
        gs = sb("gs", [P, G, E])
        top = sb("top", [P, G, 8])
        topi = sb("topi", [P, G, 8], U32)
        topf = sb("topf", [P, G, 2])
        eq = sb("eq", [P, 2, G, E])
        mk = [sb(f"mk{p}", [P, G, E]) for p in range(2)]
        mkT = sb("mkT", [E, GT], F16)
        hg = [sb(f"hg{p}", [P, NC, GT]) for p in range(2)]
        hg_hi = [sb(f"hg_hi{r}", [P, NC, GT], F16) for r in range(4)]
        hg_lo = [sb(f"hg_lo{r}", [P, NC, GT], F16) for r in range(4)]
        ym = [sb(f"ym{p}", [P, G, D]) for p in range(2)]
        acc = [sb(f"acc{p}", [P, G, D]) for p in range(2)]

        bX, bQ, bV, bO = pb("bX"), pb("bQ"), pb("bV"), pb("bO")
        bS = [pb(f"bS{j}") for j in range(2)]
        bT = [pb(f"bT{j}") for j in range(2)]

        x_in = [sem(f"x_in{k}") for k in range(XCH)]
        wa_in, wf_in, row_in, ffn_in = sem("wa_in"), sem("wf_in"), sem("row_in"), sem("ffn_in")
        adj_in = [sem(f"adj_in{p}") for p in range(2)]
        out_done = [sem("out_done0"), sem("out_done1")]
        iota_set, ident_set = sem("iota_set"), sem("ident_set")
        b_turned, b_ready = sem("b_turned"), sem("b_ready")
        prep = sem("prep")
        var_set, std_set = [sem("var0"), sem("var1")], [sem("std0"), sem("std1")]
        ln_ready = [sem("ln_ready0"), sem("ln_ready1")]
        ffn_hi_set = sem("ffn_hi_set")
        wq_scaled, wa_hi_set, wa_lo_set = sem("wq_scaled"), sem("wa_hi_set"), sem("wa_lo_set")
        mask_set, xn_mul, xn_set, xT_kept = sem("mask_set"), sem("xn_mul"), sem("xn_set"), sem("xT_kept")
        X_fill, X_hi, X_empty = sem("X_fill"), sem("X_hi"), sem("X_empty")
        Q_fill, Q_hi, Q_empty = sem("Q_fill"), sem("Q_hi"), sem("Q_empty")
        V_fill, V_hi, V_empty = sem("V_fill"), sem("V_hi"), sem("V_empty")
        O_fill, O_rden, O_empty = sem("O_fill"), sem("O_rden"), sem("O_empty")
        S_fill = [sem(f"S_fill{j}") for j in range(2)]
        half_done = [sem(f"half_done{j}") for j in range(2)]
        S_max = [sem(f"S_max{j}") for j in range(2)]
        S_empty = [sem(f"S_empty{j}") for j in range(2)]
        T_fill = [sem(f"T_fill{j}") for j in range(2)]
        T_hi = [sem(f"T_hi{j}") for j in range(2)]
        T_empty = [sem(f"T_empty{j}") for j in range(2)]
        x2_set, st_set = sem("x2_set"), sem("st_set")

        def n(bank, work, u):
            return uses(bank, work, u, UNITS)

        def later(u, k):
            return not isinstance(u, int) or u >= k

        def steps(eng, does):
            def step(i, p):
                for work, lag in ORDER:
                    if work in does and (not isinstance(i, int) or 0 <= i - lag < UNITS):
                        does[work](i - lag, (p - lag) % 2)

            for i in range(HEAD):
                step(i, i % 2)
            with eng.Fori(HEAD, UNITS - 1, 2) as i:
                step(i, 0)
                step(i + 1, 1)
            for i in range(UNITS, UNITS + LAST):
                step(i, i % 2)

        def hold(eng, tile):
            eng.tensor_tensor(tile[:, 1:2], tile[:, 0:1], tile[:, 0:1], ALU.add)

        def split3(pairs):
            for (a_hi, a_lo), (b_hi, b_lo) in pairs:
                yield a_hi, b_hi
                yield a_hi, b_lo
                yield a_lo, b_hi

        def summed(dst, pairs):
            terms = list(split3(pairs))
            for m, (a, b) in enumerate(terms):
                last = nc.tensor.matmul(dst, a, b, start=(m == 0), stop=(m == len(terms) - 1))
            return last

        with nc.Block() as block:

            @block.sync
            def _(sp):
                per = B // XCH
                for k in range(XCH):
                    sp.dma_start(xs[:, k * per:(k + 1) * per, :],
                                 x[k * per:(k + 1) * per].rearrange("b t d -> t b d")).then_inc(x_in[k], 16)
                    if k == 0:
                        for u in range(2):
                            sp.dma_start(adj_t[u][:, :, :],
                                         adj[u * U:(u + 1) * U].rearrange("b t k -> t b k")).then_inc(adj_in[u], 16)
                with sp.Fori(2, UNITS - 1, 2) as i:
                    for p in range(2):
                        sp.wait_ge(mask_set, i + p - 1)
                        sp.dma_start(adj_t[p][:, :, :],
                                     adj[bass.ds((i + p) * U, U)].rearrange("b t k -> t b k")).then_inc(adj_in[p], 16)

            @block.gpsimd
            def _(pool):
                nc.gpsimd.memset(ident[:, :], 0.0).then_inc(ident_set, 1)
                nc.gpsimd.memset(held_p[:, :], 0.0).then_inc(ident_set, 1)
                pool.wait_ge(ident_set, 2)
                nc.gpsimd.affine_select(out=ident[:, :], in_=ident[:, :], compare_op=ALU.not_equal, fill=1.0,
                                        base=0, pattern=[[-1, P]], channel_multiplier=1).then_inc(ident_set, 1)
                pool.wait_ge(ident_set, 3)
                nc.gpsimd.tensor_copy(ident_b[:, :], ident[:, :]).then_inc(ident_set, 1)
                nc.gpsimd.iota(iota8[:, :], pattern=[[1, E]], base=0, channel_multiplier=0,
                               allow_small_or_imprecise_dtypes=True).then_inc(iota_set, 1)

                pool.wait_ge(wa_hi_set, 2)
                nc.gpsimd.tensor_tensor(wa_lo[:, :, :, :].rearrange("p a b c -> p (a b c)"),
                                        wa_f[:, :, :, :].rearrange("p a b c -> p (a b c)"),
                                        wa_hi[:, :, :, :].rearrange("p a b c -> p (a b c)"),
                                        ALU.subtract).then_inc(wa_lo_set, 1)
                nc.gpsimd.tensor_tensor(wo_lo[:, :, :], wo_f[:, :, :], wo_hi[:, :, :],
                                        ALU.subtract).then_inc(wa_lo_set, 1)

                def rows_x(u, p):
                    if later(u, 2):
                        pool.wait_ge(S_fill[1], n("S", "scores1", u - 2) + 1)
                        pool.wait_ge(X_fill, n("X", "rows_x", u - 2) + 1)
                    pool.wait_ge(adj_in[p], 16 * (u // 2 + 1) if isinstance(u, int) else 8 * (u - p) + 16)
                    pool.wait_ge(ln_ready[0], 1)
                    sl = bass.ds(u * U, U)
                    nc.gpsimd.tensor_tensor(xn[p][:, :, :], xs[:, sl, :],
                                            rstd[0][:, sl].unsqueeze(2).broadcast_to([P, U, D]),
                                            ALU.mult).then_inc(xn_mul, 1)
                    nc.gpsimd.tensor_scalar(mask_b[p][:, :, :], adj_t[p][:, :, :], 0.0, MASKED,
                                            ALU.is_le, ALU.mult).then_inc(mask_set, 1)
                    pool.wait_ge(xn_mul, u + 1)
                    nc.gpsimd.tensor_tensor(xn[p][:, :, :], xn[p][:, :, :],
                                            nmr[0][:, sl].unsqueeze(2).broadcast_to([P, U, D]),
                                            ALU.add).then_inc(xn_set, 1)

                def qkv0(u, p):
                    if later(u, 2):
                        pool.wait_ge(V_fill, n("V", "output", u - 2) + 1)
                    pool.wait_ge(X_empty, n("X", "rows_x", u) + 1)
                    hold(nc.gpsimd, held_p)
                    nc.gpsimd.tensor_copy(xTk[p][:, :, :].bitcast(F32),
                                          xT[p][:, :, :].bitcast(F32)).then_inc(xT_kept, 1)

                steps(pool, {"rows_x": rows_x, "qkv0": qkv0})
                pool.wait_ge(ffn_hi_set, 4)
                nc.gpsimd.tensor_tensor(w1_lo[:, :, :], w1_f[:, :, :], w1_hi[:, :, :], ALU.subtract)
                nc.gpsimd.tensor_tensor(w2_lo[:, :, :, :].rearrange("p e c d -> p (e c) d"),
                                        w2_f[:, :, :, :].rearrange("p e c d -> p (e c) d"),
                                        w2_hi[:, :, :, :].rearrange("p e c d -> p (e c) d"), ALU.subtract)
                nc.gpsimd.tensor_tensor(wg_lo[:, :], wg_f[:, :], wg_hi[:, :], ALU.subtract)
                nc.gpsimd.tensor_tensor(b2_lo[:, :], b2_f[:, :], b2_hi[:, :], ALU.subtract)

            @block.scalar
            def _(act):
                for c, (w, b) in enumerate(((0, 0), (1, 0), (1, 1))):
                    for k, ws in enumerate(((Wq0, Wq1), (Wk0, Wk1), (Wv0, Wv1))):
                        act.dma_start(wa_f[:, c, k, :], ws[w][b * P:(b + 1) * P, :]).then_inc(wa_in, 16)
                act.dma_start(wo_f[:, :, :], Wout.rearrange("(c p) d -> p c d", p=P)).then_inc(wa_in, 16)
                for r, b in enumerate((bq0, bq1, bk0, bk1, bv0, bv1)):
                    act.dma_start(brows[r:r + 1, :], b.rearrange("(a d) -> a d", a=1)).then_inc(row_in, 16)
                act.dma_start(brows[6:6 + NB1, :], b1.rearrange("e (c p) -> (e c) p", p=P)).then_inc(row_in, 16)
                act.dma_start(bout_bc[:, :], bout.rearrange("(a d) -> a d", a=1).broadcast_to([P, D])).then_inc(wf_in, 16)
                act.dma_start(bg_bc[:, :], bg.rearrange("(a d) -> a d", a=1).broadcast_to([P, E])).then_inc(wf_in, 16)
                act.dma_start(wg_f[:, :], Wg).then_inc(ffn_in, 16)
                act.dma_start(b2_f[:, :], b2).then_inc(ffn_in, 16)
                act.dma_start(w1_f[:, :, :], W1.rearrange("e d h -> d e h")).then_inc(ffn_in, 16)
                act.dma_start(w2_f[:, :, :, :], W2.rearrange("e (c p) d -> p e c d", p=P)).then_inc(ffn_in, 16)
                scale = float(HD) ** -0.5
                act.wait_ge(wa_in, 160)
                nc.scalar.activation(wa_f[:, :, 0, :], wa_f[:, :, 0, :], ACT.Copy, scale=scale).then_inc(wq_scaled, 1)
                act.wait_ge(wq_scaled, 1)
                nc.scalar.activation(wa_hi[:, :, :, :], wa_f[:, :, :, :], ACT.Copy).then_inc(wa_hi_set, 1)
                nc.scalar.activation(wo_hi[:, :, :], wo_f[:, :, :], ACT.Copy).then_inc(wa_hi_set, 1)
                act.wait_ge(b_turned, 1)
                nc.scalar.activation(bcols[:, 0:2], bX[:, 0:2], ACT.Copy, scale=scale).then_inc(b_ready, 1)
                nc.scalar.activation(bcols[:, 2:6 + NB1], bX[:, 2:6 + NB1], ACT.Copy).then_inc(b_ready, 1)
                act.wait_ge(var_set[0], 1)
                nc.scalar.activation(rstd[0][:, :], sa[:, :], ACT.Sqrt, bias=eps_c[:, 0:1]).then_inc(std_set[0], 1)
                act.wait_ge(ffn_in, 64)
                nc.scalar.activation(w1_hi[:, :, :], w1_f[:, :, :], ACT.Copy).then_inc(ffn_hi_set, 1)
                nc.scalar.activation(w2_hi[:, :, :, :], w2_f[:, :, :, :], ACT.Copy).then_inc(ffn_hi_set, 1)
                nc.scalar.activation(wg_hi[:, :], wg_f[:, :], ACT.Copy).then_inc(ffn_hi_set, 1)
                nc.scalar.activation(b2_hi[:, :], b2_f[:, :], ACT.Copy).then_inc(ffn_hi_set, 1)
                act.wait_ge(b_ready, 2)

                def probs_hi(l, u):
                    for j in range(2):
                        act.wait_ge(T_fill[j], n("T", f"probs{l}", u) + 1)
                        nc.scalar.activation(prT_hi[l][:, j, :, :].rearrange("p a b -> p (a b)"), bT[j][:, :],
                                             ACT.Copy).then_inc(T_hi[j], 1)

                def rows_hi(dst, bias, work, u):
                    act.wait_ge(X_fill, n("X", work, u) + 1)
                    if bias is None:
                        if later(u, 2):
                            act.wait_ge(xT_kept, u - 1)
                        nc.scalar.activation(dst[:, 0, :], bX[:, 0:TOK], ACT.Copy).then_inc(X_hi, 1)
                    else:
                        nc.scalar.activation(dst[:, 0, :], bX[:, 0:TOK], ACT.Identity, bias=bias).then_inc(X_hi, 1)

                def qkv_hi(l, u):
                    act.wait_ge(Q_fill, n("Q", f"qkv{l}", u) + 1)
                    nc.scalar.activation(qT[l][:, 0, :], bQ[:, 0:TOK], ACT.Identity, bias=bq[l])
                    nc.scalar.activation(kT[l][:, 0, :], bQ[:, TOK:2 * TOK], ACT.Identity, bias=bk[l]).then_inc(Q_hi, 1)
                    act.wait_ge(V_fill, n("V", f"qkv{l}", u) + 1)
                    nc.scalar.activation(v_hi[l][:, :, :, 0:HD].rearrange("p u h d -> p (u h) d"),
                                         bV[:, 0:TOK].rearrange("p (a d) -> p a d", d=HD), ACT.Copy).then_inc(V_hi, 1)

                def exps(l, u):
                    for j in range(2):
                        act.wait_ge(S_max[j], n("S", f"scores{l}", u) + 1)
                        for a in range(2 * U):
                            last = nc.scalar.activation(pr[l][:, j, a, :], bS[j][:, a * T:(a + 1) * T], ACT.Exp,
                                                        bias=nmax[:, l, j, a:a + 1])
                        last.then_inc(S_empty[j], 1)

                steps(act, {
                    "rows_x": lambda u, p: rows_hi(xT[p], None, "rows_x", u),
                    "qkv0": lambda u, p: qkv_hi(0, u),
                    "scores0": lambda u, p: exps(0, u),
                    "probs0": lambda u, p: probs_hi(0, u),
                    "rows_h0": lambda u, p: rows_hi(h0T[p], bv[0], "rows_h0", u),
                    "qkv1": lambda u, p: qkv_hi(1, u),
                    "scores1": lambda u, p: exps(1, u),
                    "probs1": lambda u, p: probs_hi(1, u),
                    "rows_h1": lambda u, p: rows_hi(h1T, bv[1], "rows_h1", u),
                })
                act.wait_ge(var_set[1], 1)
                nc.scalar.activation(rstd[1][:, :], sa[:, :], ACT.Sqrt, bias=eps_c[:, 0:1]).then_inc(std_set[1], 1)

            @block.vector
            def _(dve):
                done = [0]

                def then_wait(ins):
                    done[0] += 1
                    ins.then_inc(prep, 1)
                    dve.wait_ge(prep, done[0])

                def layer_norm_scalars(k):
                    s = st[k]
                    nc.vector.tensor_tensor(sa[:, :], s[:, :, 1], s[:, :, 4], ALU.subtract)
                    then_wait(nc.vector.tensor_tensor(nmr[k][:, :], s[:, :, 1], s[:, :, 4], ALU.add))
                    then_wait(nc.vector.scalar_tensor_tensor(out=sbb[:, :], in0=sa[:, :], scalar=0.25, in1=sa[:, :],
                                                             op0=ALU.mult, op1=ALU.mult))
                    then_wait(nc.vector.scalar_tensor_tensor(out=sbb[:, :], in0=s[:, :, 2], scalar=1.0 / D, in1=sbb[:, :],
                                                             op0=ALU.mult, op1=ALU.add))
                    nc.vector.scalar_tensor_tensor(out=sa[:, :], in0=s[:, :, 5], scalar=1.0 / D, in1=sbb[:, :],
                                                   op0=ALU.mult, op1=ALU.add).then_inc(var_set[k], 1)
                    dve.wait_ge(std_set[k], 1)
                    then_wait(nc.vector.reciprocal(rstd[k][:, :], rstd[k][:, :]))
                    nc.vector.scalar_tensor_tensor(out=nmr[k][:, :], in0=nmr[k][:, :], scalar=-0.5, in1=rstd[k][:, :],
                                                   op0=ALU.mult, op1=ALU.mult).then_inc(ln_ready[k], 1)

                nc.vector.memset(eps_c[:, :], EPS)
                nc.vector.memset(held_v[:, :], 0.0)
                for l in range(2):
                    nc.vector.memset(v_hi[l][:, :, :, HD:HD + 1], 1.0)
                per = B // XCH
                for b in range(B):
                    if b % per == 0:
                        dve.wait_ge(x_in[b // per], 16)
                    last = nc.vector.bn_stats(st[0][:, b, :], xs[:, b, :])
                then_wait(last)
                layer_norm_scalars(0)
                dve.wait_ge(wf_in, 32)
                dve.wait_ge(b_ready, 2)

                def probs_lo(l, u):
                    for j in range(2):
                        dve.wait_ge(T_hi[j], n("T", f"probs{l}", u) + 1)
                        nc.vector.tensor_tensor(prT_lo[l][:, j, :, :].rearrange("p a b -> p (a b)"), bT[j][:, :],
                                                prT_hi[l][:, j, :, :].rearrange("p a b -> p (a b)"),
                                                ALU.subtract).then_inc(T_empty[j], 1)

                def rows_lo(dst, bias, work, u):
                    dve.wait_ge(X_hi, n("X", work, u) + 1)
                    if bias is None:
                        nc.vector.tensor_tensor(dst[:, 1, :], bX[:, 0:TOK], dst[:, 0, :],
                                                ALU.subtract).then_inc(X_empty, 1)
                    else:
                        nc.vector.scalar_tensor_tensor(out=dst[:, 1, :], in0=bX[:, 0:TOK], scalar=bias,
                                                       in1=dst[:, 0, :], op0=ALU.add,
                                                       op1=ALU.subtract).then_inc(X_empty, 1)

                def qkv_lo(l, u):
                    dve.wait_ge(Q_hi, n("Q", f"qkv{l}", u) + 1)
                    nc.vector.scalar_tensor_tensor(out=qT[l][:, 1, :], in0=bQ[:, 0:TOK], scalar=bq[l],
                                                   in1=qT[l][:, 0, :], op0=ALU.add, op1=ALU.subtract)
                    nc.vector.scalar_tensor_tensor(out=kT[l][:, 1, :], in0=bQ[:, TOK:2 * TOK], scalar=bk[l],
                                                   in1=kT[l][:, 0, :], op0=ALU.add,
                                                   op1=ALU.subtract).then_inc(Q_empty, 1)
                    dve.wait_ge(V_hi, n("VH", f"qkv{l}", u) + 1)
                    nc.vector.tensor_tensor(v_lo[l][:, :, :, :].rearrange("p u h d -> p (u h) d"),
                                            bV[:, 0:TOK].rearrange("p (a d) -> p a d", d=HD),
                                            v_hi[l][:, :, :, 0:HD].rearrange("p u h d -> p (u h) d"),
                                            ALU.subtract).then_inc(V_empty, 1)

                def maxima(l, u):
                    for j in range(2):
                        dve.wait_ge(S_fill[j], n("S", f"scores{l}", u) + 1)
                        nc.vector.tensor_reduce(nmax[:, l, j, :], bS[j][:, :].rearrange("p (a k) -> p a k", k=T),
                                                axis=AX.X, op=ALU.max, negate=True).then_inc(S_max[j], 1)

                def normalise(l, u):
                    o = bO[:, 0:U * HEADS * (HD + 1)].rearrange("p (a d) -> p a d", d=HD + 1)
                    dve.wait_ge(O_fill, n("O", f"sums{l}", u) + 1)
                    nc.vector.reciprocal(rden[:, l, :], o[:, :, HD]).then_inc(O_rden, 1)
                    dve.wait_ge(O_rden, n("O", f"sums{l}", u) + 1)
                    nc.vector.tensor_tensor(hn[l][:, :, :].rearrange("p u (h d) -> p (u h) d", d=HD), o[:, :, 0:HD],
                                            rden[:, l, :].unsqueeze(2).broadcast_to([P, U * HEADS, HD]),
                                            ALU.mult).then_inc(O_empty, 1)

                def residual(u):
                    dve.wait_ge(V_fill, n("V", "output", u) + 1)
                    nc.vector.tensor_tensor(og[:, :, :], bV[:, 0:TOK].rearrange("p (u d) -> p u d", u=U),
                                            bout_bc[:, :].unsqueeze(1).broadcast_to([P, U, D]),
                                            ALU.add).then_inc(V_empty, 1)
                    dve.wait_ge(V_empty, n("V", "output", u) + 1)
                    x_u = xs[:, bass.ds(u * U, U), :].rearrange("p u d -> p (u d)")
                    nc.vector.scalar_tensor_tensor(out=x_u, in0=og[:, :, :].rearrange("p u d -> p (u d)"), scalar=0.0,
                                                   in1=x_u, op0=ALU.max, op1=ALU.add).then_inc(x2_set, 1)
                    dve.wait_ge(x2_set, u + 1)
                    for b in range(U):
                        g = bass.ds(u * U + b, 1)
                        nc.vector.bn_stats(st[1][:, g, :].rearrange("p a s -> p (a s)"),
                                           xs[:, g, :].rearrange("p a d -> p (a d)")).then_inc(st_set, 1)

                steps(dve, {
                    "rows_x": lambda u, p: rows_lo(xT[p], None, "rows_x", u),
                    "qkv0": lambda u, p: qkv_lo(0, u),
                    "scores0": lambda u, p: maxima(0, u),
                    "probs0": lambda u, p: probs_lo(0, u),
                    "sums0": lambda u, p: normalise(0, u),
                    "rows_h0": lambda u, p: rows_lo(h0T[p], bv[0], "rows_h0", u),
                    "qkv1": lambda u, p: qkv_lo(1, u),
                    "scores1": lambda u, p: maxima(1, u),
                    "probs1": lambda u, p: probs_lo(1, u),
                    "sums1": lambda u, p: normalise(1, u),
                    "rows_h1": lambda u, p: rows_lo(h1T, bv[1], "rows_h1", u),
                    "output": lambda u, p: residual(u),
                })
                dve.wait_ge(st_set, B)
                layer_norm_scalars(1)

            @block.tensor
            def _(pe):
                pe.wait_ge(row_in, 112)
                pe.wait_ge(ident_set, 4)
                nc.tensor.transpose(bX[:, 0:6 + NB1], brows[:, :], ident[0:6 + NB1, 0:6 + NB1]).then_inc(b_turned, 1)
                pe.wait_ge(b_ready, 2)
                pe.wait_ge(wa_lo_set, 2)

                def bank_free(bank, empty, work, u):
                    count = n(bank, work, u)
                    if not isinstance(u, int) or count:
                        pe.wait_ge(empty, count)

                def turn_rows(src, ready, value, work, u):
                    pe.wait_ge(ready, value)
                    bank_free("X", X_empty, work, u)
                    for g in range(U):
                        last = nc.tensor.transpose(bX[:, g * T:(g + 1) * T], src[:, g, :], ident[:, :])
                    last.then_inc(X_fill, 1)

                def project(l, rows, rows_work, u):
                    pe.wait_ge(X_empty, n("X", rows_work, u) + 1)
                    bank_free("Q", Q_empty, f"qkv{l}", u)
                    for k in range(2):
                        last = summed(bQ[:, k * TOK:(k + 1) * TOK],
                                      [((wa_hi[:, c, k, :], wa_lo[:, c, k, :]), (r[:, 0, :], r[:, 1, :])) for c, r in rows])
                    last.then_inc(Q_fill, 1)
                    bank_free("V", V_empty, f"qkv{l}", u)
                    for g in range(U):
                        ts = slice(g * T, (g + 1) * T)
                        last = summed(bV[:, ts], [((r[:, 0, ts], r[:, 1, ts]), (wa_hi[:, c, 2, :], wa_lo[:, c, 2, :]))
                                                  for c, r in rows])
                    last.then_inc(V_fill, 1)

                def score(l, u, p):
                    work = f"scores{l}"
                    if l == 0:
                        pe.wait_ge(mask_set, u + 1)
                    pe.wait_ge(Q_empty, n("Q", f"qkv{l}", u) + 1)
                    for h in range(HEADS):
                        j, w = h % 2, h // 2
                        cols = slice(w * U * T, (w + 1) * U * T)
                        if w:
                            pe.wait_ge(half_done[j], n("S", work, u) + 1)
                        else:
                            bank_free("S", S_empty[j], work, u)
                        nc.tensor.matmul(bS[j][:, cols], ident_b[:, :],
                                         mask_b[p][:, :, :].rearrange("p u k -> p (u k)"), start=w == 0, stop=False)
                        hs = slice(h * HD, (h + 1) * HD)
                        for g in range(U):
                            ts = slice(g * T, (g + 1) * T)
                            a = w * U + g
                            for m, (qh, kh) in enumerate(((0, 0), (0, 1), (1, 0))):
                                last = nc.tensor.matmul(bS[j][:, a * T:(a + 1) * T], qT[l][hs, qh, ts],
                                                        kT[l][hs, kh, ts], start=False,
                                                        stop=m == 2 and a == 2 * U - 1)
                        last.then_inc(S_fill[j] if w else half_done[j], 1)

                def turn_probs(l, u):
                    for j in range(2):
                        pe.wait_ge(S_empty[j], n("S", f"scores{l}", u) + 1)
                        bank_free("T", T_empty[j], f"probs{l}", u)
                        for a in range(2 * U):
                            last = nc.tensor.transpose(bT[j][:, a * T:(a + 1) * T], pr[l][:, j, a, :], ident[:, :])
                        last.then_inc(T_fill[j], 1)

                def weigh(l, u):
                    bank_free("O", O_empty, f"sums{l}", u)
                    pe.wait_ge(V_empty, n("V", f"qkv{l}", u) + 1)
                    for j in range(2):
                        pe.wait_ge(T_empty[j], n("T", f"probs{l}", u) + 1)
                        for h in range(j, HEADS, 2):
                            for g in range(U):
                                a = U * (h // 2) + g
                                o = (g * HEADS + h) * (HD + 1)
                                nc.tensor.matmul(bO[:, o:o + HD + 1], prT_hi[l][:, j, a, :], v_hi[l][:, g, h, :],
                                                 start=True, stop=False)
                                nc.tensor.matmul(bO[:, o:o + HD], prT_hi[l][:, j, a, :], v_lo[l][:, g, h, :],
                                                 start=False, stop=False, skip_group_check=True)
                                last = nc.tensor.matmul(bO[:, o:o + HD + 1], prT_lo[l][:, j, a, :], v_hi[l][:, g, h, :],
                                                        start=False, stop=True)
                    last.then_inc(O_fill, 1)

                def output(u, p):
                    pe.wait_ge(X_empty, n("X", "rows_h1", u) + 1)
                    pe.wait_ge(xT_kept, u + 1)
                    bank_free("V", V_empty, "output", u)
                    for g in range(U):
                        ts = slice(g * T, (g + 1) * T)
                        last = summed(bV[:, ts], [((r[:, 0, ts], r[:, 1, ts]), (wo_hi[:, c, :], wo_lo[:, c, :]))
                                                  for c, r in enumerate((xTk[p], h0T[p], h1T))])
                    last.then_inc(V_fill, 1)

                steps(pe, {
                    "rows_x": lambda u, p: turn_rows(xn[p], xn_set, u + 1, "rows_x", u),
                    "qkv0": lambda u, p: project(0, [(0, xT[p])], "rows_x", u),
                    "scores0": lambda u, p: score(0, u, p),
                    "probs0": lambda u, p: turn_probs(0, u),
                    "sums0": lambda u, p: weigh(0, u),
                    "rows_h0": lambda u, p: turn_rows(hn[0], O_empty, n("O", "sums0", u) + 1, "rows_h0", u),
                    "qkv1": lambda u, p: project(1, [(1, xT[p]), (2, h0T[p])], "rows_h0", u),
                    "scores1": lambda u, p: score(1, u, p),
                    "probs1": lambda u, p: turn_probs(1, u),
                    "sums1": lambda u, p: weigh(1, u),
                    "rows_h1": lambda u, p: turn_rows(hn[1], O_empty, n("O", "sums1", u) + 1, "rows_h1", u),
                    "output": output,
                })

        bH = [[bQ, bV], [bO, bX]]
        bY = bS
        bR, bG = bT
        xr_mul, xr_set = sem("xr_mul"), sem("xr_set")
        R_fill, R_hi, R_empty = sem("R_fill"), sem("R_hi"), sem("R_empty")
        G_fill, G_empty = sem("G_fill"), sem("G_empty")
        chain = sem("chain")
        mk_set = sem("mk_set")
        H_fill, H_gelu, H_hi, H_lo = sem("H_fill"), sem("H_gelu"), sem("H_hi"), sem("H_lo")
        Y_fill, Y_empty = sem("Y_fill"), sem("Y_empty")
        acc_set, acc_init = sem("acc_set"), sem("acc_init")

        def groups(eng, body):
            body(-1, 1)
            body(0, 0)
            body(1, 1)
            with eng.Fori(2, GROUPS - 3, 2) as g:
                body(g, 0)
                body(g + 1, 1)
            body(GROUPS - 2, 0)
            body(GROUPS - 1, 1)

        def has(g):
            return not isinstance(g, int) or g >= 0

        def has_next(g):
            return not isinstance(g, int) or g + 1 < GROUPS

        def ahead(g, p, e, k):
            if e + k >= E:
                g, p, e = g + 1, 1 - p, e - E
            return (g, p, e + k) if not isinstance(g, int) or 0 <= g < GROUPS else None

        def later_e(g, e, k):
            return not isinstance(g, int) or g * E + e >= k

        TURN, GATE, MASKT, BIAS2 = 0, 2, 4, 6

        with nc.Block() as block:

            @block.gpsimd
            def _(pool):
                def body(g, p):
                    if has_next(g):
                        sl = bass.ds((g + 1) * G, G)
                        if has(g):
                            pool.wait_ge(R_fill, 2 * g + 1)
                        nc.gpsimd.tensor_tensor(xn2[:, :, :], xs[:, sl, :],
                                                rstd[1][:, sl].unsqueeze(2).broadcast_to([P, G, D]),
                                                ALU.mult).then_inc(xr_mul, 1)
                        pool.wait_ge(xr_mul, g + 2)
                        nc.gpsimd.tensor_tensor(xn2[:, :, :], xn2[:, :, :],
                                                nmr[1][:, sl].unsqueeze(2).broadcast_to([P, G, D]),
                                                ALU.add).then_inc(xr_set, 1)

                groups(pool, body)

            @block.sync
            def _(sp):
                def body(g, p):
                    if has(g):
                        sp.wait_ge(acc_set, (g + 1) * E)
                        sp.dma_start(out[bass.ds(g * G, G)].rearrange("b t d -> t b d"),
                                     acc[p][:, :, :]).then_inc(out_done[p], 16)

                groups(sp, body)
                for p in range(2):
                    sp.wait_ge(out_done[p], 16 * (GROUPS // 2))

            @block.scalar
            def _(act):
                def body(g, p):
                    for e in range(E):
                        if e == TURN and has_next(g):
                            act.wait_ge(R_fill, 2 * (g + 1) + 1)
                            nc.scalar.activation(x2T[1 - p][:, 0, :], bR[:, :], ACT.Copy).then_inc(R_hi, 1)
                        if ahead(g, p, e, 2):
                            hidden(*ahead(g, p, e, 2))

                def hidden(g, p, e):
                    t = g * E + e
                    act.wait_ge(H_fill, t + 1)
                    if later_e(g, e, 2):
                        act.wait_ge(H_lo, t - 1)
                    for c in range(NC):
                        col = 6 + e * NC + c
                        last = nc.scalar.activation(hg[e % 2][:, c, :], bH[e % 2][c][:, :], ACT.Gelu,
                                                    bias=bcols[:, col:col + 1])
                    last.then_inc(H_gelu, 1)
                    act.wait_ge(H_gelu, t + 1)
                    if later_e(g, e, 4):
                        act.wait_ge(Y_fill, t - 3)
                    nc.scalar.activation(hg_hi[e % 4][:, :, :], hg[e % 2][:, :, :], ACT.Copy).then_inc(H_hi, 1)

                groups(act, body)

            @block.vector
            def _(dve):
                STEPS = 4

                def body(g, p):
                    for e in range(E):
                        if has_next(g):
                            step = [STEPS * (g + 1)]

                            def then_wait(ins):
                                ins.then_inc(chain, 1)
                                step[0] = step[0] + 1
                                dve.wait_ge(chain, step[0])

                            if e == TURN:
                                dve.wait_ge(R_hi, g + 2)
                                nc.vector.tensor_tensor(x2T[1 - p][:, 1, :], bR[:, :], x2T[1 - p][:, 0, :],
                                                        ALU.subtract).then_inc(R_empty, 1)
                            if e == GATE:
                                dve.wait_ge(G_fill, 2 * (g + 1) + 1)
                                nc.vector.tensor_tensor(gs[:, :, :], bG[:, 0:G * E].rearrange("p (b e) -> p b e", e=E),
                                                        bg_bc[:, :].unsqueeze(1).broadcast_to([P, G, E]),
                                                        ALU.add).then_inc(G_empty, 1)
                                dve.wait_ge(G_empty, 2 * (g + 1) + 1)
                                hold(nc.vector, held_v)
                                for b in range(G):
                                    last = nc.vector.max(top[:, b, :], gs[:, b, :])
                                then_wait(last)
                                hold(nc.vector, held_v)
                                for b in range(G):
                                    last = nc.vector.max_index(topi[:, b, :], top[:, b, :], gs[:, b, :])
                                then_wait(last)
                                then_wait(nc.vector.tensor_copy(topf[:, :, :], topi[:, :, 0:2]))
                                for k in range(2):
                                    last = nc.vector.tensor_tensor(eq[:, k, :, :],
                                                                   iota8[:, :].unsqueeze(1).broadcast_to([P, G, E]),
                                                                   topf[:, :, k:k + 1].broadcast_to([P, G, E]), ALU.is_equal)
                                then_wait(last)
                                nc.vector.tensor_tensor(mk[1 - p][:, :, :], eq[:, 0, :, :], eq[:, 1, :, :],
                                                        ALU.add).then_inc(mk_set, 1)
                            if e == MASKT:
                                dve.wait_ge(G_fill, 2 * (g + 1) + 2)
                                nc.vector.tensor_copy(mkT[:, :], bG[0:E, :]).then_inc(G_empty, 1)
                            if e == BIAS2:
                                dve.wait_ge(R_fill, 2 * (g + 1) + 2)
                                if has(g) and (not isinstance(g, int) or g > 0):
                                    dve.wait_ge(out_done[1 - p], 8 * g + 8 * p)
                                nc.vector.tensor_tensor(acc[1 - p][:, :, :], bR[:, :].rearrange("p (b d) -> p b d", d=D),
                                                        xs[:, bass.ds((g + 1) * G, G), :], ALU.add).then_inc(R_empty, 1)
                        if ahead(g, p, e, 1):
                            low(*ahead(g, p, e, 1))
                        if has(g) and e > 0:
                            masked_add(g, p, e - 1)
                    if has(g):
                        masked_add(g, p, E - 1)

                def low(g, p, e):
                    dve.wait_ge(H_hi, g * E + e + 1)
                    nc.vector.tensor_tensor(hg_lo[e % 4][:, :, :].rearrange("p c t -> p (c t)"),
                                            hg[e % 2][:, :, :].rearrange("p c t -> p (c t)"),
                                            hg_hi[e % 4][:, :, :].rearrange("p c t -> p (c t)"),
                                            ALU.subtract).then_inc(H_lo, 1)

                def masked_add(g, p, e):
                    q = e % 2
                    ge = g * E + e
                    dve.wait_ge(Y_fill, ge + 1)
                    nc.vector.tensor_tensor(ym[q][:, :, :], bY[q][:, :].rearrange("p (b d) -> p b d", d=D),
                                            mk[p][:, :, e:e + 1].broadcast_to([P, G, D]), ALU.mult).then_inc(Y_empty, 1)
                    dve.wait_ge(Y_empty, ge + 1)
                    if e == 0:
                        dve.wait_ge(R_empty, 2 * g + 2)
                    else:
                        dve.wait_ge(acc_set, ge)
                    nc.vector.tensor_tensor(acc[p][:, :, :], acc[p][:, :, :], ym[q][:, :, :],
                                            ALU.add).then_inc(acc_set, 1)

                groups(dve, body)

            @block.tensor
            def _(pe):
                def first(g, p, e):
                    q = e % 2
                    ge = g * E + e
                    if e == 0:
                        pe.wait_ge(R_empty, 2 * g + 1)
                    if not isinstance(g, int) or g > 0 or e >= 2:
                        pe.wait_ge(H_gelu, ge - 1)
                    for c in range(NC):
                        cs = slice(c * P, (c + 1) * P)
                        last = summed(bH[q][c][:, :], [((w1_hi[:, e, cs], w1_lo[:, e, cs]),
                                                        (x2T[p][:, 0, :], x2T[p][:, 1, :]))])
                    last.then_inc(H_fill, 1)

                def second(g, p, e):
                    q = e % 2
                    ge = g * E + e
                    pe.wait_ge(H_lo, ge + 1)
                    if not isinstance(g, int) or g > 0 or e >= 2:
                        pe.wait_ge(Y_empty, ge - 1)
                    for b in range(G):
                        ts = slice(b * T, (b + 1) * T)
                        last = summed(bY[q][:, ts], [((hg_hi[e % 4][:, c, ts], hg_lo[e % 4][:, c, ts]),
                                                      (w2_hi[:, e, c, :], w2_lo[:, e, c, :])) for c in range(NC)])
                    last.then_inc(Y_fill, 1)

                def body(g, p):
                    for e in range(E):
                        if has_next(g):
                            m = 2 * (g + 1)
                            if e == TURN:
                                pe.wait_ge(xr_set, g + 2)
                                if has(g):
                                    pe.wait_ge(R_empty, m)
                                for b in range(G):
                                    last = nc.tensor.transpose(bR[:, b * T:(b + 1) * T], xn2[:, b, :], ident[:, :])
                                last.then_inc(R_fill, 1)
                            if e == GATE:
                                pe.wait_ge(R_empty, m + 1)
                                if has(g):
                                    pe.wait_ge(G_empty, m)
                                for b in range(G):
                                    ts = slice(b * T, (b + 1) * T)
                                    last = summed(bG[:, b * E:(b + 1) * E],
                                                  [((x2T[1 - p][:, 0, ts], x2T[1 - p][:, 1, ts]), (wg_hi[:, :], wg_lo[:, :]))])
                                last.then_inc(G_fill, 1)
                            if e == MASKT:
                                pe.wait_ge(mk_set, g + 2)
                                pe.wait_ge(G_empty, m + 1)
                                for b in range(G):
                                    last = nc.tensor.transpose(bG[0:E, b * T:(b + 1) * T], mk[1 - p][:, b, :], ident[:, :])
                                last.then_inc(G_fill, 1)
                            if e == BIAS2:
                                pe.wait_ge(G_empty, m + 2)
                                for b in range(G):
                                    ts = slice(b * T, (b + 1) * T)
                                    nc.tensor.matmul(bR[:, ts], mkT[:, ts], b2_hi[:, :], start=True, stop=False)
                                    last = nc.tensor.matmul(bR[:, ts], mkT[:, ts], b2_lo[:, :], start=False, stop=True)
                                last.then_inc(R_fill, 1)
                        if ahead(g, p, e, 2):
                            first(*ahead(g, p, e, 2))
                        if has(g):
                            second(g, p, e)

                groups(pe, body)


_INS = ["x", "adj", "L0_gnn_Wq0", "L0_gnn_bq0", "L0_gnn_Wk0", "L0_gnn_bk0", "L0_gnn_Wv0", "L0_gnn_bv0",
        "L0_gnn_Wq1", "L0_gnn_bq1", "L0_gnn_Wk1", "L0_gnn_bk1", "L0_gnn_Wv1", "L0_gnn_bv1",
        "L0_gnn_Wout", "L0_gnn_bout", "L0_ffn_Wg", "L0_ffn_bg", "L0_ffn_W1", "L0_ffn_b1", "L0_ffn_W2", "L0_ffn_b2"]


def kernel(**inputs):
    import numpy as np
    import concourse.bacc as bacc
    from concourse.bass_utils import run_bass_kernel_spmd

    nc = bacc.Bacc("TRN2", target_bir_lowering=False, num_devices=1)
    arrays, args = {}, []
    for name in _INS:
        a = np.ascontiguousarray(inputs[name])
        arrays[f"in_{name}"] = a
        args.append(nc.dram_tensor(f"in_{name}", a.shape, mybir.dt.from_np(a.dtype), kind="ExternalInput").ap())
    args.append(nc.dram_tensor("out", inputs["x"].shape, F32, kind="ExternalOutput").ap())
    gnn_moe_kernel(nc, *args)
    r = run_bass_kernel_spmd(nc, [arrays], core_ids=[0])
    return r.results[0]["out"]
```

```python
from contextlib import ExitStack

import concourse.bass as bass
from concourse import mybir

F32 = mybir.dt.float32
F16 = mybir.dt.float16
BF16 = mybir.dt.bfloat16
I32 = mybir.dt.int32
U32 = mybir.dt.uint32
ALU = mybir.AluOpType
ACT = mybir.ActivationFunctionType
AX = mybir.AxisListType

P = 128
HEADS = 4
EPS = 1e-5
MASKED = -(2.0 ** 100)

ORDER = (("rows_x", 0), ("output", 3), ("sums0", 1), ("qkv0", 0), ("probs1", 2), ("rows_h0", 1),
         ("scores0", 0), ("sums1", 2), ("qkv1", 1), ("rows_h1", 2), ("probs0", 0), ("scores1", 1))
LAG = dict(ORDER)
LAST = max(LAG.values())
ACT_ORDER = (("rows_x", 0), ("scores1", 2), ("qkv0", 0), ("probs1", 2), ("rows_h0", 1), ("scores0", 0),
             ("qkv1", 1), ("rows_h1", 2), ("probs0", 0))
DVE_ORDER = (("qkv1", 2), ("rows_h1", 3), ("probs0", 1), ("scores1", 2), ("rows_x", 0), ("output", 3),
             ("sums0", 1), ("qkv0", 0), ("probs1", 2), ("scores0", 0), ("rows_h0", 1), ("sums1", 2))
BANK = {"rows_x": "V", "rows_h0": "Q", "rows_h1": "X", "q0": "Q", "k0": "X", "q1": "O", "k1": "Q", "v0": "V",
        "v1": "V", "output": "X", "sums0": "O", "sums1": "V", "scores0": "S", "scores1": "S", "probs0": "T",
        "probs1": "T"}
HIGH = ("rows_x", "rows_h0", "rows_h1", "q0", "k0", "v0", "q1", "k1", "v1")


def uses(fill, u, units, high=False):
    parts = [(f, lag) for work, lag in ORDER
             for f in ([part + work[3] for part in "qkv"] if work[:3] == "qkv" else [work])]
    order = [(f, lag) for f, lag in parts if BANK[f] == BANK[fill] and (f in HIGH or not high)]
    before = [f for f, _ in order].index(fill)
    i = u + order[before][1]
    if not isinstance(u, int):
        return i * len(order) - sum(lag for _, lag in order) + before
    done = sum(min(max(i - lag, 0), units) for _, lag in order)
    return done + sum(0 <= i - lag < units for _, lag in order[:before])


def gnn_moe_kernel(nc, x, adj, Wq0, bq0, Wk0, bk0, Wv0, bv0, Wq1, bq1, Wk1, bk1, Wv1, bv1,
                   Wout, bout, Wg, bg, W1, b1, W2, b2, out):
    B, T, D = x.shape
    E, _, HID = W1.shape
    assert T == P and D == P and HID == 2 * P and B % 8 == 0
    HD = D // HEADS
    U = 2
    UNITS = B // U
    TOK = U * T
    NC = HID // P
    NB1 = E * NC
    G = 4
    GROUPS = B // G
    GT = G * T
    XCH = 8
    RING = 4
    HEAD = 2 * RING
    assert UNITS % RING == 0 and LAST <= RING and HEAD < UNITS
    per = B // XCH
    LN_ENDS = ((2 * U, 2 * per, B), (B - 2 * G, B))
    assert 2 * U <= per and HEAD * U <= 2 * per < B and LN_ENDS[1][0] <= B - LAST * U and LN_ENDS[1][0] % G == 0

    with ExitStack() as ctx:
        def sb(name, shape, dt=F32):
            return ctx.enter_context(nc.sbuf_tensor(name, shape, dt))

        def pb(name, shape=(P, 512), dt=F32):
            return ctx.enter_context(nc.psum_tensor(name, list(shape), dt))

        def sem(name):
            return ctx.enter_context(nc.semaphore(name))

        ident = sb("ident", [P, P])
        ident_b = sb("ident_b", [P, P], BF16)
        iota8 = sb("iota8", [P, E])
        brows = sb("brows", [6 + NB1, P])
        bcols = sb("bcols", [P, 6 + NB1])
        bq = [bcols[:, 0:1], bcols[:, 1:2]]
        bk = [bcols[:, 2:3], bcols[:, 3:4]]
        bv = [bcols[:, 4:5], bcols[:, 5:6]]
        bout_bc = sb("bout_bc", [P, D])
        bg_bc = sb("bg_bc", [P, E])
        b2_f = sb("b2_f", [E, D])
        b2_hi = sb("b2_hi", [E, D], F16)
        b2_lo = sb("b2_lo", [E, D], BF16)
        wa_f = sb("wa_f", [P, 3, 3, D])
        wa_hi = sb("wa_hi", [P, 3, 3, D], F16)
        wa_lo = sb("wa_lo", [P, 3, 3, D], BF16)
        wo_f = sb("wo_f", [P, 3, D])
        wo_hi = sb("wo_hi", [P, 3, D], F16)
        wo_lo = sb("wo_lo", [P, 3, D], BF16)
        wg_f = sb("wg_f", [P, E])
        wg_hi = sb("wg_hi", [P, E], F16)
        wg_lo = sb("wg_lo", [P, E], BF16)
        w1_f = sb("w1_f", [P, E, HID])
        w1_hi = sb("w1_hi", [P, E, HID], F16)
        w1_lo = sb("w1_lo", [P, E, HID], BF16)
        w2_f = sb("w2_f", [P, E, NC, D])
        w2_hi = sb("w2_hi", [P, E, NC, D], F16)
        w2_lo = sb("w2_lo", [P, E, NC, D], BF16)

        held_v = sb("held_v", [P, 2])

        xs = sb("xs", [P, B, D])
        st = [sb("st0", [P, B, 6]), sb("st1", [P, B, 6])]
        rstd = [sb("rstd0", [P, B]), sb("rstd1", [P, B])]
        nmr = [sb("nmr0", [P, B]), sb("nmr1", [P, B])]
        sa = sb("sa", [P, B])
        sbb = sb("sbb", [P, B])
        eps_c = sb("eps_c", [P, 1])
        sqrt_warm = sb("sqrt_warm", [P, 1])
        xn2 = sb("xn2", [P, G, D])

        gnn = ctx.enter_context(ExitStack())

        def ring(depth, name, shape, dt=F32):
            return [gnn.enter_context(nc.sbuf_tensor(f"{name}_{r}", shape, dt)) for r in range(depth)] * (RING // depth)

        adj_t = ring(2, "adj", [P, U, T], I32)
        mask_b = ring(4, "mask", [P, U, T], BF16)
        xn = ring(2, "xn", [P, U, D])
        xT = ring(4, "xT", [P, 2, TOK], F16)
        h0T = ring(4, "h0T", [P, 2, TOK], F16)
        h1T = ring(2, "h1T", [P, 2, TOK], F16)
        qT = [ring(2, f"q{l}T", [P, 2, TOK], F16) for l in range(2)]
        kT = [ring(2, f"k{l}T", [P, 2, TOK], F16) for l in range(2)]
        v_hi = [ring(4, f"v{l}_hi", [P, U, HEADS, HD + 1], F16) for l in range(2)]
        v_lo = [ring(4, f"v{l}_lo", [P, U, HEADS, HD], F16) for l in range(2)]
        pr = [ring(2, f"pr{l}", [P, 2, 2 * U, T]) for l in range(2)]
        prT_hi = [ring(2, f"pr{l}T_hi", [P, 2, 2 * U, T], F16) for l in range(2)]
        prT_lo = [ring(2, f"pr{l}T_lo", [P, 2, 2 * U, T], F16) for l in range(2)]
        nmax = [ring(2, f"nmax{l}", [P, 2, 2 * U]) for l in range(2)]
        rden = [ring(2, f"rden{l}", [P, U * HEADS]) for l in range(2)]
        hn = [ring(2, f"hn{l}", [P, U, D]) for l in range(2)]
        og = ring(2, "og", [P, U, D])

        bank = {name: pb("b" + name) for name in "XQVO"}
        bS = [pb(f"bS{j}") for j in range(2)]
        bT = [pb(f"bT{j}") for j in range(2)]

        def bank_of(filled):
            return bank[BANK[filled]]

        x_first = sem("x_first")
        x_in = [sem(f"x_in{k}") for k in range(XCH)]
        wa0_in, wa1_in, wf_in, row_in, ffn_in = sem("wa0_in"), sem("wa1_in"), sem("wf_in"), sem("row_in"), sem("ffn_in")
        adj_in = [sem(f"adj_in{r}") for r in range(2)]
        out_done = [sem("out_done0"), sem("out_done1")]
        iota_set, ident_set = sem("iota_set"), sem("ident_set")
        b_turned, b_ready = sem("b_turned"), sem("b_ready")
        prep = sem("prep")
        var_set, std_set = [sem("var0"), sem("var1")], [sem("std0"), sem("std1")]
        ln_ready = [sem("ln_ready0"), sem("ln_ready1")]
        ffn_hi_set = sem("ffn_hi_set")
        wq_scaled = sem("wq_scaled")
        wa_hi_set, wa_lo_set = [sem("wa0_hi"), sem("wa1_hi")], [sem("wa0_lo"), sem("wa1_lo")]
        eps_set, xr_mul, xr_set = sem("eps_set"), sem("xr_mul"), sem("xr_set")
        mask_set, xn_mul, xn_set = sem("mask_set"), sem("xn_mul"), sem("xn_set")
        fill, hi, empty = [{name: sem(f"{name}_{what}") for name in "XQVO"} for what in ("fill", "hi", "empty")]
        rden_set = sem("rden_set")
        S_fill = [sem(f"S_fill{j}") for j in range(2)]
        half_done = [sem(f"half_done{j}") for j in range(2)]
        S_max = [sem(f"S_max{j}") for j in range(2)]
        S_empty = [sem(f"S_empty{j}") for j in range(2)]
        T_fill = [sem(f"T_fill{j}") for j in range(2)]
        T_hi = [sem(f"T_hi{j}") for j in range(2)]
        T_empty = [sem(f"T_empty{j}") for j in range(2)]
        x2_set, st_set = sem("x2_set"), sem("st_set")

        def n(filled, u):
            return uses(filled, u, UNITS)

        def n_high(filled, u):
            return uses(filled, u, UNITS, high=True)

        def later(u, k):
            return not isinstance(u, int) or u >= k

        def steps(eng, order, does, also={}):
            def step(i, at):
                if isinstance(i, int) and i in also:
                    also[i]()
                for work, lag in order:
                    if work in does and (not isinstance(i, int) or 0 <= i - lag < UNITS):
                        does[work](i - lag, (at - lag) % RING)

            for i in range(HEAD):
                step(i, i)
            with eng.Fori(HEAD, UNITS - RING + 1, RING) as i:
                for k in range(RING):
                    step(i + k, k)
            for i in range(UNITS, UNITS + max(lag for _, lag in order)):
                step(i, i)

        def hold(eng, tile):
            eng.tensor_tensor(tile[:, 1:2], tile[:, 0:1], tile[:, 0:1], ALU.add)

        def split3(pairs):
            for (a_hi, a_lo), (b_hi, b_lo) in pairs:
                yield a_hi, b_hi
                yield a_hi, b_lo
                yield a_lo, b_hi

        def summed(dst, pairs):
            terms = list(split3(pairs))
            for m, (a, b) in enumerate(terms):
                last = nc.tensor.matmul(dst, a, b, start=(m == 0), stop=(m == len(terms) - 1))
            return last

        prep_done = [0]

        def then_wait(dve, ins):
            prep_done[0] += 1
            ins.then_inc(prep, 1)
            dve.wait_ge(prep, prep_done[0])

        def ln_graphs(k, part):
            return (0, *LN_ENDS[k])[part], LN_ENDS[k][part]

        def layer_norm_sums(dve, k, part):
            s, cut = st[k], slice(*ln_graphs(k, part))
            nc.vector.tensor_tensor(sa[:, cut], s[:, cut, 1], s[:, cut, 4], ALU.subtract)
            then_wait(dve, nc.vector.tensor_tensor(nmr[k][:, cut], s[:, cut, 1], s[:, cut, 4], ALU.add))
            then_wait(dve, nc.vector.scalar_tensor_tensor(out=sbb[:, cut], in0=sa[:, cut], scalar=0.25, in1=sa[:, cut],
                                                          op0=ALU.mult, op1=ALU.mult))
            then_wait(dve, nc.vector.scalar_tensor_tensor(out=sbb[:, cut], in0=s[:, cut, 2], scalar=1.0 / D,
                                                          in1=sbb[:, cut], op0=ALU.mult, op1=ALU.add))
            nc.vector.scalar_tensor_tensor(out=sa[:, cut], in0=s[:, cut, 5], scalar=1.0 / D, in1=sbb[:, cut],
                                           op0=ALU.mult, op1=ALU.add).then_inc(var_set[k], 1)

        def layer_norm_root(act, k, part):
            lo, hi = ln_graphs(k, part)
            act.wait_ge(var_set[k], part + 1)
            nc.scalar.activation(rstd[k][:, lo:hi], sa[:, lo:hi], ACT.Sqrt, bias=eps_c[:, 0:1]).then_inc(std_set[k], 1)

        def layer_norm_scalars(dve, k, part):
            lo, hi = ln_graphs(k, part)
            dve.wait_ge(std_set[k], part + 1)
            then_wait(dve, nc.vector.reciprocal(rstd[k][:, lo:hi], rstd[k][:, lo:hi]))
            nc.vector.scalar_tensor_tensor(out=nmr[k][:, lo:hi], in0=nmr[k][:, lo:hi], scalar=-0.5, in1=rstd[k][:, lo:hi],
                                           op0=ALU.mult, op1=ALU.mult).then_inc(ln_ready[k], 1)

        def normalised_rows(pool, g):
            sl = bass.ds(g * G, G)
            nc.gpsimd.tensor_tensor(xn2[:, :, :], xs[:, sl, :],
                                    rstd[1][:, sl].unsqueeze(2).broadcast_to([P, G, D]), ALU.mult).then_inc(xr_mul, 1)
            pool.wait_ge(xr_mul, g + 1)
            nc.gpsimd.tensor_tensor(xn2[:, :, :], xn2[:, :, :],
                                    nmr[1][:, sl].unsqueeze(2).broadcast_to([P, G, D]), ALU.add).then_inc(xr_set, 1)

        with nc.Block() as block:

            @block.sync
            def _(sp):
                def x_chunk(k):
                    sp.dma_start(xs[:, k * per:(k + 1) * per, :],
                                 x[k * per:(k + 1) * per].rearrange("b t d -> t b d")).then_inc(x_in[k], 16)

                def adjacency(u):
                    sp.dma_start(adj_t[u][:, :, :],
                                 adj[u * U:(u + 1) * U].rearrange("b t k -> t b k")).then_inc(adj_in[u], 16)

                sp.dma_start(xs[:, 0:2 * U, :], x[0:2 * U].rearrange("b t d -> t b d")).then_inc(x_first, 16)
                adjacency(0)
                sp.dma_start(xs[:, 2 * U:per, :], x[2 * U:per].rearrange("b t d -> t b d")).then_inc(x_in[0], 16)
                for r, b in enumerate((bq0, bq1, bk0, bk1, bv0, bv1)):
                    sp.dma_start(brows[r:r + 1, :], b.rearrange("(a d) -> a d", a=1)).then_inc(row_in, 16)
                sp.dma_start(brows[6:6 + NB1, :], b1.rearrange("e (c p) -> (e c) p", p=P)).then_inc(row_in, 16)
                x_chunk(1)
                for k, w in enumerate((Wq1, Wk1, Wv1)):
                    sp.dma_start(wa_f[:, 1:3, k, :], w.rearrange("(c p) d -> p c d", p=P)).then_inc(wa1_in, 16)
                adjacency(1)
                sp.dma_start(wo_f[:, :, :], Wout.rearrange("(c p) d -> p c d", p=P)).then_inc(wa1_in, 16)
                sp.dma_start(bout_bc[:, :], bout.rearrange("(a d) -> a d", a=1).broadcast_to([P, D])).then_inc(wf_in, 16)
                sp.dma_start(bg_bc[:, :], bg.rearrange("(a d) -> a d", a=1).broadcast_to([P, E])).then_inc(wf_in, 16)
                for k in range(2, XCH):
                    x_chunk(k)
                sp.dma_start(wg_f[:, :], Wg).then_inc(ffn_in, 16)
                sp.dma_start(b2_f[:, :], b2).then_inc(ffn_in, 16)
                sp.dma_start(w1_f[:, :, :], W1.rearrange("e d h -> d e h")).then_inc(ffn_in, 16)
                sp.dma_start(w2_f[:, :, :, :], W2.rearrange("e (c p) d -> p e c d", p=P)).then_inc(ffn_in, 16)
                with sp.Fori(2, UNITS - 1, 2) as i:
                    for p in range(2):
                        sp.wait_ge(mask_set, i + (p - 1))
                        sp.dma_start(adj_t[p][:, :, :],
                                     adj[bass.ds((i + p) * U, U)].rearrange("b t k -> t b k")).then_inc(adj_in[p], 16)

            @block.gpsimd
            def _(pool):
                nc.gpsimd.memset(ident[:, :], 0.0).then_inc(ident_set, 1)
                pool.wait_ge(ident_set, 1)
                nc.gpsimd.affine_select(out=ident[:, :], in_=ident[:, :], compare_op=ALU.not_equal, fill=1.0,
                                        base=0, pattern=[[-1, P]], channel_multiplier=1).then_inc(ident_set, 1)
                pool.wait_ge(ident_set, 2)
                nc.gpsimd.tensor_copy(ident_b[:, :], ident[:, :]).then_inc(ident_set, 1)
                nc.gpsimd.iota(iota8[:, :], pattern=[[1, E]], base=0, channel_multiplier=0,
                               allow_small_or_imprecise_dtypes=True).then_inc(iota_set, 1)

                def layer_1_weights():
                    pool.wait_ge(wa_hi_set[1], 2)
                    nc.gpsimd.tensor_tensor(wa_lo[:, 1:3, :, :].rearrange("p a b c -> p (a b c)"),
                                            wa_f[:, 1:3, :, :].rearrange("p a b c -> p (a b c)"),
                                            wa_hi[:, 1:3, :, :].rearrange("p a b c -> p (a b c)"),
                                            ALU.subtract).then_inc(wa_lo_set[1], 1)
                    nc.gpsimd.tensor_tensor(wo_lo[:, :, :], wo_f[:, :, :], wo_hi[:, :, :],
                                            ALU.subtract).then_inc(wa_lo_set[1], 1)

                def rows_x(u, r):
                    if later(u, 4):
                        pool.wait_ge(S_fill[1], n("scores1", u - 4) + 1)
                    if later(u, 2):
                        pool.wait_ge(fill[BANK["rows_x"]], n("rows_x", u - 2) + 1)
                    pool.wait_ge(adj_in[r % 2], 16 * (u // 2 + 1) if isinstance(u, int) else 8 * (u - r % 2) + 16)
                    pool.wait_ge(ln_ready[0], 3 if not isinstance(u, int) else
                                 1 + sum((u + 1) * U > end for end in LN_ENDS[0]))
                    sl = bass.ds(u * U, U)
                    nc.gpsimd.tensor_tensor(xn[r][:, :, :], xs[:, sl, :],
                                            rstd[0][:, sl].unsqueeze(2).broadcast_to([P, U, D]),
                                            ALU.mult).then_inc(xn_mul, 1)
                    nc.gpsimd.tensor_scalar(mask_b[r][:, :, :], adj_t[r][:, :, :], 0.0, MASKED,
                                            ALU.is_le, ALU.mult).then_inc(mask_set, 1)
                    pool.wait_ge(xn_mul, u + 1)
                    nc.gpsimd.tensor_tensor(xn[r][:, :, :], xn[r][:, :, :],
                                            nmr[0][:, sl].unsqueeze(2).broadcast_to([P, U, D]),
                                            ALU.add).then_inc(xn_set, 1)

                steps(pool, (("rows_x", 0),), {"rows_x": rows_x}, {1: layer_1_weights})
                pool.wait_ge(ffn_hi_set, 10)
                nc.gpsimd.tensor_tensor(w1_lo[:, :, :], w1_f[:, :, :], w1_hi[:, :, :], ALU.subtract)
                nc.gpsimd.tensor_tensor(w2_lo[:, :, :, :].rearrange("p e c d -> p (e c) d"),
                                        w2_f[:, :, :, :].rearrange("p e c d -> p (e c) d"),
                                        w2_hi[:, :, :, :].rearrange("p e c d -> p (e c) d"), ALU.subtract)
                nc.gpsimd.tensor_tensor(wg_lo[:, :], wg_f[:, :], wg_hi[:, :], ALU.subtract)
                nc.gpsimd.tensor_tensor(b2_lo[:, :], b2_f[:, :], b2_hi[:, :], ALU.subtract)
                pool.wait_ge(ln_ready[1], 1)
                normalised_rows(pool, 0)

            @block.scalar
            def _(act):
                for k, w in enumerate((Wq0, Wk0, Wv0)):
                    act.dma_start(wa_f[:, 0, k, :], w).then_inc(wa0_in, 16)
                act.wait_ge(eps_set, 1)
                nc.scalar.activation(sqrt_warm[:, :], eps_c[:, :], ACT.Sqrt, bias=eps_c[:, 0:1])
                layer_norm_root(act, 0, 0)
                scale = float(HD) ** -0.5
                act.wait_ge(wa0_in, 48)
                nc.scalar.activation(wa_f[:, 0, 0, :], wa_f[:, 0, 0, :], ACT.Copy, scale=scale).then_inc(wq_scaled, 1)
                act.wait_ge(wq_scaled, 1)
                nc.scalar.activation(wa_hi[:, 0, :, :], wa_f[:, 0, :, :], ACT.Copy).then_inc(wa_hi_set[0], 1)
                act.wait_ge(b_turned, 1)
                nc.scalar.activation(bcols[:, 0:2], bank["X"][:, 0:2], ACT.Copy, scale=scale).then_inc(b_ready, 1)
                nc.scalar.activation(bcols[:, 2:6 + NB1], bank["X"][:, 2:6 + NB1], ACT.Copy).then_inc(b_ready, 1)
                act.wait_ge(b_ready, 2)

                def layer_1_weights():
                    act.wait_ge(wa1_in, 64)
                    nc.scalar.activation(wa_f[:, 1:3, 0, :], wa_f[:, 1:3, 0, :], ACT.Copy,
                                         scale=scale).then_inc(wq_scaled, 1)
                    act.wait_ge(wq_scaled, 2)
                    nc.scalar.activation(wa_hi[:, 1:3, :, :], wa_f[:, 1:3, :, :], ACT.Copy).then_inc(wa_hi_set[1], 1)
                    nc.scalar.activation(wo_hi[:, :, :], wo_f[:, :, :], ACT.Copy).then_inc(wa_hi_set[1], 1)

                def ffn_weights(part):
                    es = slice(part * (E // 4), (part + 1) * (E // 4))
                    if part == 0:
                        act.wait_ge(ffn_in, 64)
                        nc.scalar.activation(wg_hi[:, :], wg_f[:, :], ACT.Copy).then_inc(ffn_hi_set, 1)
                        nc.scalar.activation(b2_hi[:, :], b2_f[:, :], ACT.Copy).then_inc(ffn_hi_set, 1)
                    nc.scalar.activation(w1_hi[:, es, :], w1_f[:, es, :], ACT.Copy).then_inc(ffn_hi_set, 1)
                    nc.scalar.activation(w2_hi[:, es, :, :], w2_f[:, es, :, :], ACT.Copy).then_inc(ffn_hi_set, 1)

                def probs_hi(l, u, r):
                    for j in range(2):
                        act.wait_ge(T_fill[j], n(f"probs{l}", u) + 1)
                        nc.scalar.activation(prT_hi[l][r][:, j, :, :].rearrange("p a b -> p (a b)"), bT[j][:, :],
                                             ACT.Copy).then_inc(T_hi[j], 1)

                def rows_hi(dst, bias, work, u):
                    if work == "rows_h1" and isinstance(u, int) and u == UNITS - 1:
                        layer_norm_root(act, 1, 0)
                    act.wait_ge(fill[BANK[work]], n(work, u) + 1)
                    src = bank_of(work)[:, 0:TOK]
                    if bias is None:
                        nc.scalar.activation(dst[:, 0, :], src, ACT.Copy).then_inc(hi[BANK[work]], 1)
                        if isinstance(u, int) and u == 0:
                            layer_1_weights()
                            layer_norm_root(act, 0, 1)
                    else:
                        nc.scalar.activation(dst[:, 0, :], src, ACT.Identity, bias=bias).then_inc(hi[BANK[work]], 1)

                def qkv_hi(l, u, r):
                    q, k, v = f"q{l}", f"k{l}", f"v{l}"
                    for f, dst, bias in ((q, qT, bq), (k, kT, bk)):
                        act.wait_ge(fill[BANK[f]], n(f, u) + 1)
                        nc.scalar.activation(dst[l][r][:, 0, :], bank_of(f)[:, 0:TOK], ACT.Identity,
                                             bias=bias[l]).then_inc(hi[BANK[f]], 1)
                    act.wait_ge(fill[BANK[v]], n(v, u) + 1)
                    nc.scalar.activation(v_hi[l][r][:, :, :, 0:HD].rearrange("p u h d -> p (u h) d"),
                                         bank_of(v)[:, 0:TOK].rearrange("p (a d) -> p a d", d=HD),
                                         ACT.Copy).then_inc(hi[BANK[v]], 1)

                def exps(l, u, r):
                    for j in range(2):
                        act.wait_ge(S_max[j], n(f"scores{l}", u) + 1)
                        for a in range(2 * U):
                            last = nc.scalar.activation(pr[l][r][:, j, a, :], bS[j][:, a * T:(a + 1) * T], ACT.Exp,
                                                        bias=nmax[l][r][:, j, a:a + 1])
                        last.then_inc(S_empty[j], 1)

                steps(act, ACT_ORDER, {
                    "rows_x": lambda u, r: rows_hi(xT[r], None, "rows_x", u),
                    "qkv0": lambda u, r: qkv_hi(0, u, r),
                    "scores0": lambda u, r: exps(0, u, r),
                    "probs0": lambda u, r: probs_hi(0, u, r),
                    "rows_h0": lambda u, r: rows_hi(h0T[r], bv[0], "rows_h0", u),
                    "qkv1": lambda u, r: qkv_hi(1, u, r),
                    "scores1": lambda u, r: exps(1, u, r),
                    "probs1": lambda u, r: probs_hi(1, u, r),
                    "rows_h1": lambda u, r: rows_hi(h1T[r], bv[1], "rows_h1", u),
                }, {
                    **{HEAD - 2: lambda: layer_norm_root(act, 0, 2)},
                    **{2 + part: lambda part=part: ffn_weights(part) for part in range(4)},
                })

            @block.vector
            def _(dve):
                def row_statistics(lo, hi):
                    for b in range(lo, hi):
                        if b == 0:
                            dve.wait_ge(x_first, 16)
                        elif b == 2 * U:
                            dve.wait_ge(x_in[0], 16)
                        elif b % per == 0:
                            dve.wait_ge(x_in[b // per], 16)
                        last = nc.vector.bn_stats(st[0][:, b, :], xs[:, b, :])
                    if hi in LN_ENDS[0]:
                        then_wait(dve, last)

                nc.vector.memset(eps_c[:, :], EPS).then_inc(eps_set, 1)
                nc.vector.memset(held_v[:, :], 0.0)
                for l in range(2):
                    for r in range(4):
                        nc.vector.memset(v_hi[l][r][:, :, :, HD:HD + 1], 1.0)
                row_statistics(0, LN_ENDS[0][0])
                layer_norm_sums(dve, 0, 0)
                row_statistics(LN_ENDS[0][0], per)
                layer_norm_scalars(dve, 0, 0)
                dve.wait_ge(wa_hi_set[0], 1)
                nc.vector.tensor_tensor(wa_lo[:, 0, :, :], wa_f[:, 0, :, :], wa_hi[:, 0, :, :],
                                        ALU.subtract).then_inc(wa_lo_set[0], 1)
                dve.wait_ge(b_ready, 2)
                pieces = HEAD - 3
                cut = [2 * per + (B - 2 * per) * k // pieces for k in range(pieces + 1)]

                def before_step(k):
                    if k == 0:
                        layer_norm_scalars(dve, 0, 1)
                    if k < pieces:
                        row_statistics(cut[k], cut[k + 1])
                    if k == pieces - 1:
                        layer_norm_sums(dve, 0, 2)
                    if k == pieces + 1:
                        layer_norm_scalars(dve, 0, 2)
                    if k == 1:
                        dve.wait_ge(wf_in, 32)

                def probs_lo(l, u, r):
                    if l == 1 and isinstance(u, int) and u == UNITS - 1:
                        dve.wait_ge(st_set, LN_ENDS[1][0])
                        layer_norm_sums(dve, 1, 0)
                    for j in range(2):
                        dve.wait_ge(T_hi[j], n(f"probs{l}", u) + 1)
                        nc.vector.tensor_tensor(prT_lo[l][r][:, j, :, :].rearrange("p a b -> p (a b)"), bT[j][:, :],
                                                prT_hi[l][r][:, j, :, :].rearrange("p a b -> p (a b)"),
                                                ALU.subtract).then_inc(T_empty[j], 1)

                def rows_lo(dst, bias, work, u):
                    if work == "rows_h1" and isinstance(u, int) and u == UNITS - 1:
                        layer_norm_scalars(dve, 1, 0)
                    dve.wait_ge(hi[BANK[work]], n_high(work, u) + 1)
                    src = bank_of(work)[:, 0:TOK]
                    if bias is None:
                        nc.vector.tensor_tensor(dst[:, 1, :], src, dst[:, 0, :],
                                                ALU.subtract).then_inc(empty[BANK[work]], 1)
                        if isinstance(u, int) and u == 0:
                            row_statistics(per, LN_ENDS[0][1])
                            layer_norm_sums(dve, 0, 1)
                    else:
                        nc.vector.scalar_tensor_tensor(out=dst[:, 1, :], in0=src, scalar=bias, in1=dst[:, 0, :],
                                                       op0=ALU.add, op1=ALU.subtract).then_inc(empty[BANK[work]], 1)

                def qkv_lo(l, u, r):
                    q, k, v = f"q{l}", f"k{l}", f"v{l}"
                    for f, dst, bias in ((q, qT, bq), (k, kT, bk)):
                        dve.wait_ge(hi[BANK[f]], n_high(f, u) + 1)
                        nc.vector.scalar_tensor_tensor(out=dst[l][r][:, 1, :], in0=bank_of(f)[:, 0:TOK],
                                                       scalar=bias[l], in1=dst[l][r][:, 0, :], op0=ALU.add,
                                                       op1=ALU.subtract).then_inc(empty[BANK[f]], 1)
                    dve.wait_ge(hi[BANK[v]], n_high(v, u) + 1)
                    nc.vector.tensor_tensor(v_lo[l][r][:, :, :, :].rearrange("p u h d -> p (u h) d"),
                                            bank_of(v)[:, 0:TOK].rearrange("p (a d) -> p a d", d=HD),
                                            v_hi[l][r][:, :, :, 0:HD].rearrange("p u h d -> p (u h) d"),
                                            ALU.subtract).then_inc(empty[BANK[v]], 1)

                def maxima(l, u, r):
                    for j in range(2):
                        dve.wait_ge(S_fill[j], n(f"scores{l}", u) + 1)
                        nc.vector.tensor_reduce(nmax[l][r][:, j, :], bS[j][:, :].rearrange("p (a k) -> p a k", k=T),
                                                axis=AX.X, op=ALU.max, negate=True).then_inc(S_max[j], 1)

                def normalised(l, u):
                    lag, both = dict(DVE_ORDER), [w for w, _ in DVE_ORDER if w in ("sums0", "sums1")]
                    i = u + lag[f"sums{l}"]
                    before = both.index(f"sums{l}")
                    if not isinstance(u, int):
                        return 2 * i - lag["sums0"] - lag["sums1"] + before
                    return (sum(min(max(i - lag[w], 0), UNITS) for w in both) +
                            sum(0 <= i - lag[w] < UNITS for w in both[:before]))

                def normalise(l, u, r):
                    work = f"sums{l}"
                    o = bank_of(work)[:, 0:U * HEADS * (HD + 1)].rearrange("p (a d) -> p a d", d=HD + 1)
                    dve.wait_ge(fill[BANK[work]], n(work, u) + 1)
                    nc.vector.reciprocal(rden[l][r][:, :], o[:, :, HD]).then_inc(rden_set, 1)
                    dve.wait_ge(rden_set, normalised(l, u) + 1)
                    nc.vector.tensor_tensor(hn[l][r][:, :, :].rearrange("p u (h d) -> p (u h) d", d=HD), o[:, :, 0:HD],
                                            rden[l][r][:, :].unsqueeze(2).broadcast_to([P, U * HEADS, HD]),
                                            ALU.mult).then_inc(empty[BANK[work]], 1)

                def residual(u, r):
                    dve.wait_ge(fill[BANK["output"]], n("output", u) + 1)
                    nc.vector.tensor_tensor(og[r][:, :, :], bank_of("output")[:, 0:TOK].rearrange("p (u d) -> p u d", u=U),
                                            bout_bc[:, :].unsqueeze(1).broadcast_to([P, U, D]),
                                            ALU.add).then_inc(empty[BANK["output"]], 1)
                    dve.wait_ge(empty[BANK["output"]], n("output", u) + 1)
                    x_u = xs[:, bass.ds(u * U, U), :].rearrange("p u d -> p (u d)")
                    nc.vector.scalar_tensor_tensor(out=x_u, in0=og[r][:, :, :].rearrange("p u d -> p (u d)"), scalar=0.0,
                                                   in1=x_u, op0=ALU.max, op1=ALU.add).then_inc(x2_set, 1)
                    dve.wait_ge(x2_set, u + 1)
                    for b in range(U):
                        g = bass.ds(u * U + b, 1)
                        nc.vector.bn_stats(st[1][:, g, :].rearrange("p a s -> p (a s)"),
                                           xs[:, g, :].rearrange("p a d -> p (a d)")).then_inc(st_set, 1)

                steps(dve, DVE_ORDER, {
                    "rows_x": lambda u, r: rows_lo(xT[r], None, "rows_x", u),
                    "qkv0": lambda u, r: qkv_lo(0, u, r),
                    "scores0": lambda u, r: maxima(0, u, r),
                    "probs0": lambda u, r: probs_lo(0, u, r),
                    "sums0": lambda u, r: normalise(0, u, r),
                    "rows_h0": lambda u, r: rows_lo(h0T[r], bv[0], "rows_h0", u),
                    "qkv1": lambda u, r: qkv_lo(1, u, r),
                    "scores1": lambda u, r: maxima(1, u, r),
                    "probs1": lambda u, r: probs_lo(1, u, r),
                    "sums1": lambda u, r: normalise(1, u, r),
                    "rows_h1": lambda u, r: rows_lo(h1T[r], bv[1], "rows_h1", u),
                    "output": residual,
                }, {
                    **{k + 1: lambda k=k: before_step(k) for k in range(pieces + 2)},
                })

            @block.tensor
            def _(pe):
                pe.wait_ge(row_in, 112)
                pe.wait_ge(ident_set, 3)
                nc.tensor.transpose(bank["X"][:, 0:6 + NB1], brows[:, :], ident[0:6 + NB1, 0:6 + NB1]).then_inc(b_turned, 1)
                pe.wait_ge(b_ready, 2)

                def bank_free(work, u, empty_of=empty):
                    count = n(work, u)
                    if not isinstance(u, int) or count:
                        pe.wait_ge(empty_of[BANK[work]], count)

                def turn_rows(src, ready, value, work, u):
                    pe.wait_ge(ready, value)
                    bank_free(work, u)
                    for g in range(U):
                        last = nc.tensor.transpose(bank_of(work)[:, g * T:(g + 1) * T], src[:, g, :], ident[:, :])
                    last.then_inc(fill[BANK[work]], 1)

                def project(l, rows, rows_work, u, r):
                    if isinstance(u, int) and u == 0:
                        pe.wait_ge(wa_lo_set[l], l + 1)
                    q, k, v = f"q{l}", f"k{l}", f"v{l}"
                    for j, f in enumerate((q, k)):
                        bank_free(f, u)
                        for m, (c, w) in enumerate(rows):
                            newest = j == 0 and m == len(rows) - 1
                            if newest:
                                pe.wait_ge(hi[BANK[rows_work]], n_high(rows_work, u) + 1)
                            dst = bank_of(f)[:, 0:TOK]
                            nc.tensor.matmul(dst, wa_hi[:, c, j, :], w[:, 0, :], start=m == 0, stop=False)
                            nc.tensor.matmul(dst, wa_lo[:, c, j, :], w[:, 0, :], start=False, stop=False)
                            if newest:
                                pe.wait_ge(empty[BANK[rows_work]], n(rows_work, u) + 1)
                            last = nc.tensor.matmul(dst, wa_hi[:, c, j, :], w[:, 1, :], start=False,
                                                    stop=m == len(rows) - 1)
                        last.then_inc(fill[BANK[f]], 1)
                    bank_free(v, u)
                    for g in range(U):
                        ts = slice(g * T, (g + 1) * T)
                        last = summed(bank_of(v)[:, ts],
                                      [((w[:, 0, ts], w[:, 1, ts]), (wa_hi[:, c, 2, :], wa_lo[:, c, 2, :]))
                                       for c, w in rows])
                    last.then_inc(fill[BANK[v]], 1)

                def score(l, u, r):
                    work = f"scores{l}"
                    if l == 0:
                        pe.wait_ge(mask_set, u + 1)

                    def add_mask(h):
                        nc.tensor.matmul(bS[h % 2][:, h // 2 * U * T:(h // 2 + 1) * U * T], ident_b[:, :],
                                         mask_b[r][:, :, :].rearrange("p u k -> p (u k)"), start=h < 2, stop=False)

                    def add_products(h, passes):
                        hs = slice(h * HD, (h + 1) * HD)
                        for g in range(U):
                            ts = slice(g * T, (g + 1) * T)
                            a = h // 2 * U + g
                            for qh, kh in passes:
                                last = nc.tensor.matmul(bS[h % 2][:, a * T:(a + 1) * T], qT[l][r][hs, qh, ts],
                                                        kT[l][r][hs, kh, ts], start=False,
                                                        stop=(qh, kh) == (1, 0) and a == 2 * U - 1)
                        return last

                    bank_free(work, u, {"S": S_empty[0]})
                    for f in (f"q{l}", f"k{l}"):
                        pe.wait_ge(hi[BANK[f]], n_high(f, u) + 1)
                    add_mask(0)
                    add_products(0, ((0, 0),))
                    bank_free(work, u, {"S": S_empty[1]})
                    for f in (f"q{l}", f"k{l}"):
                        pe.wait_ge(empty[BANK[f]], n(f, u) + 1)
                    add_mask(1)
                    add_products(0, ((0, 1), (1, 0))).then_inc(half_done[0], 1)
                    add_products(1, ((0, 0), (0, 1), (1, 0))).then_inc(half_done[1], 1)
                    for h in (2, 3):
                        pe.wait_ge(half_done[h - 2], n(work, u) + 1)
                        add_mask(h)
                        add_products(h, ((0, 0), (0, 1), (1, 0))).then_inc(S_fill[h - 2], 1)

                def turn_probs(l, u, r):
                    for j in range(2):
                        pe.wait_ge(S_empty[j], n(f"scores{l}", u) + 1)
                        bank_free(f"probs{l}", u, {"T": T_empty[j]})
                        for a in range(2 * U):
                            last = nc.tensor.transpose(bT[j][:, a * T:(a + 1) * T], pr[l][r][:, j, a, :], ident[:, :])
                        last.then_inc(T_fill[j], 1)

                def weigh(l, u, r):
                    work = f"sums{l}"
                    bank_free(work, u)
                    pe.wait_ge(empty[BANK[f"v{l}"]], n(f"v{l}", u) + 1)
                    for j in range(2):
                        pe.wait_ge(T_empty[j], n(f"probs{l}", u) + 1)
                        for h in range(j, HEADS, 2):
                            for g in range(U):
                                a = U * (h // 2) + g
                                o = (g * HEADS + h) * (HD + 1)
                                nc.tensor.matmul(bank_of(work)[:, o:o + HD + 1], prT_hi[l][r][:, j, a, :], v_hi[l][r][:, g, h, :],
                                                 start=True, stop=False)
                                nc.tensor.matmul(bank_of(work)[:, o:o + HD], prT_hi[l][r][:, j, a, :], v_lo[l][r][:, g, h, :],
                                                 start=False, stop=False, skip_group_check=True)
                                last = nc.tensor.matmul(bank_of(work)[:, o:o + HD + 1], prT_lo[l][r][:, j, a, :], v_hi[l][r][:, g, h, :],
                                                        start=False, stop=True)
                    last.then_inc(fill[BANK[work]], 1)

                def output(u, r):
                    bank_free("output", u)
                    for g in range(U):
                        ts = slice(g * T, (g + 1) * T)
                        dst = bank_of("output")[:, ts]
                        for c, w in enumerate((xT[r], h0T[r], h1T[r])):
                            newest = g == 0 and c == 2
                            if newest:
                                pe.wait_ge(hi[BANK["rows_h1"]], n_high("rows_h1", u) + 1)
                            nc.tensor.matmul(dst, w[:, 0, ts], wo_hi[:, c, :], start=c == 0, stop=False)
                            nc.tensor.matmul(dst, w[:, 0, ts], wo_lo[:, c, :], start=False, stop=False)
                            if newest:
                                pe.wait_ge(empty[BANK["rows_h1"]], n("rows_h1", u) + 1)
                            last = nc.tensor.matmul(dst, w[:, 1, ts], wo_hi[:, c, :], start=False, stop=c == 2)
                    last.then_inc(fill[BANK["output"]], 1)

                steps(pe, ORDER, {
                    "rows_x": lambda u, r: turn_rows(xn[r], xn_set, u + 1, "rows_x", u),
                    "qkv0": lambda u, r: project(0, [(0, xT[r])], "rows_x", u, r),
                    "scores0": lambda u, r: score(0, u, r),
                    "probs0": lambda u, r: turn_probs(0, u, r),
                    "sums0": lambda u, r: weigh(0, u, r),
                    "rows_h0": lambda u, r: turn_rows(hn[0][r], empty[BANK["sums0"]], n("sums0", u) + 1, "rows_h0", u),
                    "qkv1": lambda u, r: project(1, [(1, xT[r]), (2, h0T[r])], "rows_h0", u, r),
                    "scores1": lambda u, r: score(1, u, r),
                    "probs1": lambda u, r: turn_probs(1, u, r),
                    "sums1": lambda u, r: weigh(1, u, r),
                    "rows_h1": lambda u, r: turn_rows(hn[1][r], empty[BANK["sums1"]], n("sums1", u) + 1, "rows_h1", u),
                    "output": output,
                })

        gnn.close()

        x2T = [sb(f"x2T{p}", [P, 2, GT], F16) for p in range(2)]
        gs = sb("gs", [P, G, E])
        top = sb("top", [P, G, 8])
        topi = sb("topi", [P, G, 8], U32)
        topf = sb("topf", [P, G, 2])
        eq = sb("eq", [P, 2, G, E])
        mk = [sb(f"mk{p}", [P, G, E]) for p in range(2)]
        mkT = sb("mkT", [E, GT], F16)
        hg = [sb(f"hg{p}", [P, NC, GT]) for p in range(2)]
        hg_hi = [sb(f"hg_hi{r}", [P, NC, GT], F16) for r in range(4)]
        hg_lo = [sb(f"hg_lo{r}", [P, NC, GT], F16) for r in range(4)]
        acc = [sb(f"acc{p}", [P, G, D]) for p in range(2)]

        bH = [[bank["Q"], bank["V"]], [bank["O"], bank["X"]]]
        bY = bS
        bR, bG = bT
        R_fill, R_hi, R_empty = sem("R_fill"), sem("R_hi"), sem("R_empty")
        G_fill, G_empty = sem("G_fill"), sem("G_empty")
        chain = sem("chain")
        mk_set = sem("mk_set")
        H_fill, H_gelu, H_hi, H_lo = sem("H_fill"), sem("H_gelu"), sem("H_hi"), sem("H_lo")
        Y_fill, acc_set = sem("Y_fill"), sem("acc_set")

        def groups(eng, body):
            body(-1, 1)
            body(0, 0)
            body(1, 1)
            with eng.Fori(2, GROUPS - 3, 2) as g:
                body(g, 0)
                body(g + 1, 1)
            body(GROUPS - 2, 0)
            body(GROUPS - 1, 1)

        def has(g):
            return not isinstance(g, int) or g >= 0

        def has_next(g):
            return not isinstance(g, int) or g + 1 < GROUPS

        def ahead(g, p, e, k):
            if e + k >= E:
                g, p, e = g + 1, 1 - p, e - E
            return (g, p, e + k) if not isinstance(g, int) or 0 <= g < GROUPS else None

        def later_e(g, e, k):
            return not isinstance(g, int) or g * E + e >= k

        TURN, GATE, TOP, MASK, MASKT, BIAS2 = 0, 2, 3, 4, 5, 6

        with nc.Block() as block:

            @block.gpsimd
            def _(pool):
                def body(g, p):
                    if has(g) and has_next(g):
                        pool.wait_ge(R_fill, 2 * g + 1)
                        if not isinstance(g, int) or (g + 1) * G >= LN_ENDS[1][0]:
                            pool.wait_ge(ln_ready[1], 2)
                        normalised_rows(pool, g + 1)

                groups(pool, body)

            @block.sync
            def _(sp):
                def body(g, p):
                    if has(g):
                        sp.wait_ge(acc_set, (g + 1) * E)
                        sp.dma_start(out[bass.ds(g * G, G)].rearrange("b t d -> t b d"),
                                     acc[p][:, :, :]).then_inc(out_done[p], 16)

                groups(sp, body)
                for p in range(2):
                    sp.wait_ge(out_done[p], 16 * (GROUPS // 2))

            @block.scalar
            def _(act):
                def body(g, p):
                    for e in range(E):
                        if e == TURN and has_next(g):
                            act.wait_ge(R_fill, 2 * (g + 1) + 1)
                            nc.scalar.activation(x2T[1 - p][:, 0, :], bR[:, :], ACT.Copy).then_inc(R_hi, 1)
                            if not has(g):
                                layer_norm_root(act, 1, 1)
                        if e == MASKT and has_next(g):
                            act.wait_ge(G_fill, 2 * (g + 1) + 2)
                            nc.scalar.activation(mkT[:, :], bG[0:E, :], ACT.Copy).then_inc(G_empty, 1)
                        if ahead(g, p, e, 2):
                            hidden(*ahead(g, p, e, 2))

                def hidden(g, p, e):
                    t = g * E + e
                    act.wait_ge(H_fill, t + 1)
                    if later_e(g, e, 2):
                        act.wait_ge(H_lo, t - 1)
                    for c in range(NC):
                        col = 6 + e * NC + c
                        last = nc.scalar.activation(hg[e % 2][:, c, :], bH[e % 2][c][:, :], ACT.Gelu,
                                                    bias=bcols[:, col:col + 1])
                    last.then_inc(H_gelu, 1)
                    act.wait_ge(H_gelu, t + 1)
                    if later_e(g, e, 4):
                        act.wait_ge(Y_fill, t - 3)
                    nc.scalar.activation(hg_hi[e % 4][:, :, :], hg[e % 2][:, :, :], ACT.Copy).then_inc(H_hi, 1)

                groups(act, body)

            @block.vector
            def _(dve):
                STEPS = 4

                def body(g, p):
                    for e in range(E):
                        if has_next(g):
                            def then_wait(step, ins):
                                ins.then_inc(chain, 1)
                                dve.wait_ge(chain, STEPS * (g + 1) + step)

                            if e == TURN:
                                dve.wait_ge(R_hi, g + 2)
                                nc.vector.tensor_tensor(x2T[1 - p][:, 1, :], bR[:, :], x2T[1 - p][:, 0, :],
                                                        ALU.subtract).then_inc(R_empty, 1)
                                if not has(g):
                                    dve.wait_ge(st_set, B)
                                    layer_norm_sums(dve, 1, 1)
                            if e == GATE:
                                dve.wait_ge(G_fill, 2 * (g + 1) + 1)
                                nc.vector.tensor_tensor(gs[:, :, :], bG[:, 0:G * E].rearrange("p (b e) -> p b e", e=E),
                                                        bg_bc[:, :].unsqueeze(1).broadcast_to([P, G, E]),
                                                        ALU.add).then_inc(G_empty, 1)
                                dve.wait_ge(G_empty, 2 * (g + 1) + 1)
                                hold(nc.vector, held_v)
                                for b in range(G):
                                    last = nc.vector.max(top[:, b, :], gs[:, b, :])
                                last.then_inc(chain, 1)
                            if e == TOP:
                                dve.wait_ge(chain, STEPS * (g + 1) + 1)
                                hold(nc.vector, held_v)
                                for b in range(G):
                                    last = nc.vector.max_index(topi[:, b, :], top[:, b, :], gs[:, b, :])
                                last.then_inc(chain, 1)
                            if e == MASK:
                                dve.wait_ge(chain, STEPS * (g + 1) + 2)
                                then_wait(3, nc.vector.tensor_copy(topf[:, :, :], topi[:, :, 0:2]))
                                for k in range(2):
                                    last = nc.vector.tensor_tensor(eq[:, k, :, :],
                                                                   iota8[:, :].unsqueeze(1).broadcast_to([P, G, E]),
                                                                   topf[:, :, k:k + 1].broadcast_to([P, G, E]), ALU.is_equal)
                                then_wait(4, last)
                                nc.vector.tensor_tensor(mk[1 - p][:, :, :], eq[:, 0, :, :], eq[:, 1, :, :],
                                                        ALU.add).then_inc(mk_set, 1)
                            if e == MASKT:
                                if not has(g):
                                    layer_norm_scalars(dve, 1, 1)
                            if e == BIAS2:
                                dve.wait_ge(R_fill, 2 * (g + 1) + 2)
                                if has(g) and (not isinstance(g, int) or g > 0):
                                    dve.wait_ge(out_done[1 - p], 8 * g + 8 * p)
                                nc.vector.tensor_tensor(acc[1 - p][:, :, :], bR[:, :].rearrange("p (b d) -> p b d", d=D),
                                                        xs[:, bass.ds((g + 1) * G, G), :], ALU.add).then_inc(R_empty, 1)
                        if ahead(g, p, e, 1):
                            low(*ahead(g, p, e, 1))
                        if has(g) and e > 0:
                            masked_add(g, p, e - 1)
                    if has(g):
                        masked_add(g, p, E - 1)

                def low(g, p, e):
                    dve.wait_ge(H_hi, g * E + e + 1)
                    nc.vector.tensor_tensor(hg_lo[e % 4][:, :, :].rearrange("p c t -> p (c t)"),
                                            hg[e % 2][:, :, :].rearrange("p c t -> p (c t)"),
                                            hg_hi[e % 4][:, :, :].rearrange("p c t -> p (c t)"),
                                            ALU.subtract).then_inc(H_lo, 1)

                def masked_add(g, p, e):
                    q = e % 2
                    ge = g * E + e
                    dve.wait_ge(Y_fill, ge + 1)
                    if e == 0:
                        dve.wait_ge(R_empty, 2 * g + 2)
                    else:
                        dve.wait_ge(acc_set, ge)
                    for b in range(G):
                        last = nc.vector.scalar_tensor_tensor(out=acc[p][:, b, :], in0=bY[q][:, b * D:(b + 1) * D],
                                                              scalar=mk[p][:, b, e:e + 1], in1=acc[p][:, b, :],
                                                              op0=ALU.mult, op1=ALU.add)
                    last.then_inc(acc_set, 1)

                groups(dve, body)

            @block.tensor
            def _(pe):
                def first(g, p, e):
                    q = e % 2
                    ge = g * E + e
                    if e == 0:
                        pe.wait_ge(R_empty, 2 * g + 1)
                    if not isinstance(g, int) or g > 0 or e >= 2:
                        pe.wait_ge(H_gelu, ge - 1)
                    for c in range(NC):
                        cs = slice(c * P, (c + 1) * P)
                        last = summed(bH[q][c][:, :], [((w1_hi[:, e, cs], w1_lo[:, e, cs]),
                                                        (x2T[p][:, 0, :], x2T[p][:, 1, :]))])
                    last.then_inc(H_fill, 1)

                def second(g, p, e):
                    q = e % 2
                    ge = g * E + e
                    pe.wait_ge(H_lo, ge + 1)
                    if not isinstance(g, int) or g > 0 or e >= 2:
                        pe.wait_ge(acc_set, ge - 1)
                    for b in range(G):
                        ts = slice(b * T, (b + 1) * T)
                        last = summed(bY[q][:, ts], [((hg_hi[e % 4][:, c, ts], hg_lo[e % 4][:, c, ts]),
                                                      (w2_hi[:, e, c, :], w2_lo[:, e, c, :])) for c in range(NC)])
                    last.then_inc(Y_fill, 1)

                def body(g, p):
                    for e in range(E):
                        if has_next(g):
                            m = 2 * (g + 1)
                            if e == TURN:
                                pe.wait_ge(xr_set, g + 2)
                                if has(g):
                                    pe.wait_ge(R_empty, m)
                                for b in range(G):
                                    last = nc.tensor.transpose(bR[:, b * T:(b + 1) * T], xn2[:, b, :], ident[:, :])
                                last.then_inc(R_fill, 1)
                            if e == GATE:
                                pe.wait_ge(R_empty, m + 1)
                                if has(g):
                                    pe.wait_ge(G_empty, m)
                                for b in range(G):
                                    ts = slice(b * T, (b + 1) * T)
                                    last = summed(bG[:, b * E:(b + 1) * E],
                                                  [((x2T[1 - p][:, 0, ts], x2T[1 - p][:, 1, ts]), (wg_hi[:, :], wg_lo[:, :]))])
                                last.then_inc(G_fill, 1)
                            if e == MASKT:
                                pe.wait_ge(mk_set, g + 2)
                                pe.wait_ge(G_empty, m + 1)
                                for b in range(G):
                                    last = nc.tensor.transpose(bG[0:E, b * T:(b + 1) * T], mk[1 - p][:, b, :], ident[:, :])
                                last.then_inc(G_fill, 1)
                            if e == BIAS2:
                                pe.wait_ge(G_empty, m + 2)
                                for b in range(G):
                                    ts = slice(b * T, (b + 1) * T)
                                    nc.tensor.matmul(bR[:, ts], mkT[:, ts], b2_hi[:, :], start=True, stop=False)
                                    last = nc.tensor.matmul(bR[:, ts], mkT[:, ts], b2_lo[:, :], start=False, stop=True)
                                last.then_inc(R_fill, 1)
                        if has(g) and ahead(g, p, e, 2):
                            first(*ahead(g, p, e, 2))
                        if not has(g) and e in (GATE, MASKT):
                            first(0, 0, 0 if e == GATE else 1)
                        if has(g):
                            second(g, p, e)

                groups(pe, body)


_INS = ["x", "adj", "L0_gnn_Wq0", "L0_gnn_bq0", "L0_gnn_Wk0", "L0_gnn_bk0", "L0_gnn_Wv0", "L0_gnn_bv0",
        "L0_gnn_Wq1", "L0_gnn_bq1", "L0_gnn_Wk1", "L0_gnn_bk1", "L0_gnn_Wv1", "L0_gnn_bv1",
        "L0_gnn_Wout", "L0_gnn_bout", "L0_ffn_Wg", "L0_ffn_bg", "L0_ffn_W1", "L0_ffn_b1", "L0_ffn_W2", "L0_ffn_b2"]


def kernel(**inputs):
    import numpy as np
    import concourse.bacc as bacc
    from concourse.bass_utils import run_bass_kernel_spmd

    nc = bacc.Bacc("TRN2", target_bir_lowering=False, num_devices=1)
    arrays, args = {}, []
    for name in _INS:
        a = np.ascontiguousarray(inputs[name])
        arrays[f"in_{name}"] = a
        args.append(nc.dram_tensor(f"in_{name}", a.shape, mybir.dt.from_np(a.dtype), kind="ExternalInput").ap())
    args.append(nc.dram_tensor("out", inputs["x"].shape, F32, kind="ExternalOutput").ap())
    gnn_moe_kernel(nc, *args)
    r = run_bass_kernel_spmd(nc, [arrays], core_ids=[0])
    return r.results[0]["out"]
```
